# Optimizing a Trainium2 kernel written in Bass

```python
import numpy as np
import jax
import jax.numpy as jnp

def _softmax(x, axis=-1):
    return jax.nn.softmax(x, axis=axis)
def _gelu(x):
    return jax.nn.gelu(x, approximate=True)
def _silu(x):
    return jax.nn.silu(x)
def _sigmoid(x):
    return jax.nn.sigmoid(x)
def _layernorm(x, axis=-1, eps=1e-5):
    m = jnp.mean(x, axis=axis, keepdims=True)
    v = jnp.var(x, axis=axis, keepdims=True)
    return (x - m) / jnp.sqrt(v + eps)
def _scatter_add(tgt, idx, src, axis=0):
    return tgt.at[idx].add(src)
def _segment_sum(src, seg, n):
    return jax.ops.segment_sum(src, seg, n)

kernel_name = 'mk_metaformer_d1_conv_nhwc128_5be36a'

def setup_inputs(seed: int = 0):
    np.random.seed(seed)
    _w = jnp.asarray
    def _rec_inputs():
        import jax
        import jax.numpy as jnp
        _gk = jax.random.key(seed)
        x = -0.000125 + 0.9999 * jax.random.normal(jax.random.fold_in(_gk, 1), (1, 512, 512, 128), jnp.float32)
        return x
    x = _rec_inputs()
    def _L0_conv_setup():
        import jax, jax.numpy as jnp
        import numpy as np
        EPS = 1e-05

        def _ln(x, g, b):
            m = jnp.mean(x, axis=-1, keepdims=True)
            v = jnp.var(x, axis=-1, keepdims=True)
            return (x - m) / jnp.sqrt(v + EPS) * g + b
        key = jax.random.key(seed)
        ks = jax.random.split(key, 16)
        B, N, CZ, C = (1, 512, 128, 16)
        s_cz = 1.0 / np.sqrt(CZ)
        s_c = 1.0 / np.sqrt(C)

        def lin(k, fan_in, shape):
            return jax.random.uniform(k, shape, jnp.float32, -1.0, 1.0) / np.sqrt(fan_in)
        return {'x': jax.random.normal(ks[0], (B, N, N, CZ), jnp.float32), 'Wa1': lin(ks[1], CZ, (CZ, C)), 'ba1': lin(ks[2], CZ, (C,)), 'Wa2': lin(ks[3], CZ, (CZ, C)), 'ba2': lin(ks[4], CZ, (C,)), 'Wb1': lin(ks[5], CZ, (CZ, C)), 'bb1': lin(ks[6], CZ, (C,)), 'Wb2': lin(ks[7], CZ, (CZ, C)), 'bb2': lin(ks[8], CZ, (C,)), 'ln2_g': jnp.ones((C,), jnp.float32), 'ln2_b': jnp.zeros((C,), jnp.float32), 'Wg': lin(ks[9], CZ, (CZ, CZ)), 'bg': lin(ks[10], CZ, (CZ,)), 'Wz': lin(ks[11], C, (C, CZ)), 'bz': lin(ks[12], C, (CZ,))}
    _L0_conv_all = _L0_conv_setup()
    _L0_conv_in = {k: v for k, v in _L0_conv_all.items() if k in ('Wa1', 'ba1', 'Wa2', 'ba2', 'Wb1', 'bb1', 'Wb2', 'bb2', 'ln2_g', 'ln2_b', 'Wg', 'bg', 'Wz', 'bz', )}
    del _L0_conv_all

    def _L0_ffn_setup():
        import jax, jax.numpy as jnp
        import numpy as np
        B, S, D, E, H, O, K = (512, 2048, 128, 64, 512, 128, 8)
        key = jax.random.key(seed)
        k0, k1, k2, k3 = jax.random.split(key, 4)
        x = jax.random.normal(k0, (B, S, D), dtype=jnp.float32)
        gate_w = jax.random.normal(k1, (E, D), dtype=jnp.float32) * (1.0 / np.sqrt(D))
        gate_b = jnp.zeros((E,), dtype=jnp.float32)
        weight1 = jax.random.uniform(k2, (E, D + 1, H), dtype=jnp.float32, minval=-1.0, maxval=1.0) * (1.0 / np.sqrt(D + 1))
        weight2 = jax.random.uniform(k3, (E, H + 1, O), dtype=jnp.float32, minval=-1.0, maxval=1.0) * (1.0 / np.sqrt(H + 1))
        return {'x': x, 'gate_w': gate_w, 'gate_b': gate_b, 'weight1': weight1, 'weight2': weight2}
    _L0_ffn_all = _L0_ffn_setup()
    _L0_ffn_in = {k: v for k, v in _L0_ffn_all.items() if k in ('gate_w', 'gate_b', 'weight1', 'weight2', )}
    del _L0_ffn_all

    return {
        "x": x,
        "L0_conv_Wa1": _L0_conv_in["Wa1"],
        "L0_conv_ba1": _L0_conv_in["ba1"],
        "L0_conv_Wa2": _L0_conv_in["Wa2"],
        "L0_conv_ba2": _L0_conv_in["ba2"],
        "L0_conv_Wb1": _L0_conv_in["Wb1"],
        "L0_conv_bb1": _L0_conv_in["bb1"],
        "L0_conv_Wb2": _L0_conv_in["Wb2"],
        "L0_conv_bb2": _L0_conv_in["bb2"],
        "L0_conv_ln2_g": _L0_conv_in["ln2_g"],
        "L0_conv_ln2_b": _L0_conv_in["ln2_b"],
        "L0_conv_Wg": _L0_conv_in["Wg"],
        "L0_conv_bg": _L0_conv_in["bg"],
        "L0_conv_Wz": _L0_conv_in["Wz"],
        "L0_conv_bz": _L0_conv_in["bz"],
        "L0_ffn_gate_w": _L0_ffn_in["gate_w"],
        "L0_ffn_gate_b": _L0_ffn_in["gate_b"],
        "L0_ffn_weight1": _L0_ffn_in["weight1"],
        "L0_ffn_weight2": _L0_ffn_in["weight2"],
    }

def reference(x, L0_conv_Wa1, L0_conv_ba1, L0_conv_Wa2, L0_conv_ba2, L0_conv_Wb1, L0_conv_bb1, L0_conv_Wb2, L0_conv_bb2, L0_conv_ln2_g, L0_conv_ln2_b, L0_conv_Wg, L0_conv_bg, L0_conv_Wz, L0_conv_bz, L0_ffn_gate_w, L0_ffn_gate_b, L0_ffn_weight1, L0_ffn_weight2):
    import jax
    import jax.numpy as jnp
    def _L0_conv_ref(x, Wa1, ba1, Wa2, ba2, Wb1, bb1, Wb2, bb2, ln2_g, ln2_b, Wg, bg, Wz, bz):
        import jax, jax.numpy as jnp
        import numpy as np
        EPS = 1e-05

        def _ln(x, g, b):
            m = jnp.mean(x, axis=-1, keepdims=True)
            v = jnp.var(x, axis=-1, keepdims=True)
            return (x - m) / jnp.sqrt(v + EPS) * g + b
        direction = 'outgoing'
        a = jax.nn.sigmoid((x @ Wa1 + ba1) * (x @ Wa2 + ba2))
        b = jax.nn.sigmoid((x @ Wb1 + bb1) * (x @ Wb2 + bb2))
        if direction == 'incoming':
            a = jnp.swapaxes(a, 1, 2)
            b = jnp.swapaxes(b, 1, 2)
        g = jax.nn.sigmoid(x @ Wg + bg)
        z = jnp.einsum('bikc,bkjc->bijc', a, b)
        return g * (_ln(z, ln2_g, ln2_b) @ Wz + bz)

    def _L0_ffn_ref(x, gate_w, gate_b, weight1, weight2):
        import jax, jax.numpy as jnp
        import numpy as np
        B, S, D, E, H, O, K = (512, 2048, 128, 64, 512, 128, 8)
        Bn, Sn, Dn = x.shape
        logits = jnp.einsum('bsd,ed->bse', x, gate_w) + gate_b
        probs = jax.nn.softmax(logits, axis=1)
        vals, idx = jax.lax.top_k(probs.transpose(0, 2, 1), K)
        topv = vals.transpose(0, 2, 1)
        topi = idx.transpose(0, 2, 1)
        flat_idx = topi.reshape(Bn, K * E)
        gathered = jnp.take_along_axis(x, flat_idx[:, :, None], axis=1)
        gathered = gathered.reshape(Bn, K, E, Dn)
        pooled = jnp.einsum('bked,bke->bed', gathered, topv)
        ones = jnp.ones((E, Bn, 1), dtype=x.dtype)
        h = jnp.concatenate([pooled.transpose(1, 0, 2), ones], axis=-1)
        h = jax.nn.gelu(jnp.einsum('ebd,edh->ebh', h, weight1), approximate=False)
        h = jnp.concatenate([h, ones], axis=-1)
        out = jnp.einsum('ebh,eho->ebo', h, weight2)
        out = out.transpose(1, 0, 2)
        weighted = jnp.einsum('beo,bke->bkeo', out, topv).reshape(Bn, K * E, O)
        outputs = jnp.zeros((Bn, Sn, O), dtype=x.dtype)
        outputs = outputs.at[jnp.arange(Bn)[:, None], flat_idx].add(weighted)
        return outputs

    def _gn(v, G=32, eps=1e-5):
        B_, H_, W_, C_ = v.shape
        g = v.reshape(B_, H_, W_, G, C_ // G)
        m = jnp.mean(g, axis=(1, 2, 4), keepdims=True)
        s = jnp.var(g, axis=(1, 2, 4), keepdims=True)
        return ((g - m) / jnp.sqrt(s + eps)).reshape(v.shape)

    def _ln_c(v, eps=1e-6):
        m = jnp.mean(v, axis=-1, keepdims=True)
        s = jnp.var(v, axis=-1, keepdims=True)
        return (v - m) / jnp.sqrt(s + eps)

    def _ln_t(v, eps=1e-5):
        m = jnp.mean(v, axis=-1, keepdims=True)
        s = jnp.var(v, axis=-1, keepdims=True)
        return (v - m) / jnp.sqrt(s + eps)

    def _to_tokens(v):
        B_, H_, W_, C_ = v.shape
        return v.reshape(B_, H_ * W_, C_)
    def _from_tokens(t, like):
        return t.reshape(like.shape)

    x = x + _L0_conv_ref(_ln_c(x), L0_conv_Wa1, L0_conv_ba1, L0_conv_Wa2, L0_conv_ba2, L0_conv_Wb1, L0_conv_bb1, L0_conv_Wb2, L0_conv_bb2, L0_conv_ln2_g, L0_conv_ln2_b, L0_conv_Wg, L0_conv_bg, L0_conv_Wz, L0_conv_bz)
    t = _to_tokens(x)
    t = t + _L0_ffn_ref(_ln_t(t), L0_ffn_gate_w, L0_ffn_gate_b, L0_ffn_weight1, L0_ffn_weight2)
    x = _from_tokens(t, x)
    return x


_drawn_inputs = setup_inputs


def setup_inputs(seed=0):
    import zlib

    import numpy as np

    out = dict(_drawn_inputs(seed))
    spreads = {'L0_conv_ln2_g': (1.0, 0.2), 'L0_conv_ln2_b': (0.0, 0.326), 'L0_ffn_gate_b': (0.0, 0.1)}
    factors = {'L0_conv_ba2': 3.431,
     'L0_conv_bb2': 3.527,
     'L0_conv_bg': 8.0,
     'L0_ffn_gate_w': 8.0,
     'L0_ffn_weight1': 8.0,
     'L0_ffn_weight2': 8.0}
    for name, (base, spread) in spreads.items():
        noise = np.random.default_rng([zlib.crc32(name.encode()), seed]).standard_normal(out[name].shape)
        drawn = base * np.exp(spread * noise) if base else spread * noise
        out[name] = jnp.asarray(drawn.astype(out[name].dtype))
    for name, factor in factors.items():
        out[name] = (out[name] * factor).astype(out[name].dtype)
    return out
```

```python
import math
from contextlib import ExitStack

import concourse.bass as bass
from concourse import mybir

F32 = mybir.dt.float32
I32 = mybir.dt.int32
U32 = mybir.dt.uint32
ALU = mybir.AluOpType
ACT = mybir.ActivationFunctionType
AX = mybir.AxisListType

P = 128
CZ = 128
C = 16
E = 64
HID = 512
K = 8
EPS_C = 1e-6
EPS_T = 1e-5
RSQRT_MAGIC = 0x5F3759DF

GT = 8
GU = 8
BATCH = 4
BT = BATCH * GT

QT = 4
QU = 8
RT = QU * QT
QB2 = 4
SLAB = 256


def since(eng, sem, value):
    if not (isinstance(value, int) and value <= 0):
        eng.wait_ge(sem, value)


def build(nc, x, Wa1, ba1, Wa2, ba2, Wb1, bb1, Wb2, bb2, ln2_g, ln2_b, Wg, bg, Wz, bz,
          gate_w, gate_b, weight1, weight2, out):
    N = x.shape[1]
    LN = N.bit_length() - 1
    NBLK = N // P
    GB = N // GT
    NG = NBLK * GB
    LGB = GB.bit_length() - 1
    NQ = NG * GT // QT
    QB = N // QT
    LQB = QB.bit_length() - 1
    NSLAB = NBLK * (N // SLAB)
    SB = N // SLAB
    LSB = SB.bit_length() - 1
    QS = SLAB // QT
    RS = QS // QU
    NROUND = NQ // QU
    NBATCH = NG // BATCH
    NW = 4 * C + CZ + E
    EG = 8
    EC = E // EG
    NCH = NG

    x_groups = x[0].rearrange("(b p) (g s) c -> b g p s c", p=P, s=GT)
    x_quads = x[0].rearrange("(b p) (g s) c -> b g p s c", p=P, s=QT)
    out_quads = out[0].rearrange("(b p) (g s) c -> b g p s c", p=P, s=QT)
    out_rows = out[0].rearrange("i j c -> (i j) c")

    a_dram = nc.dram_tensor("a_dram", (NBATCH, P, C, BT), F32, kind="Internal").ap()
    a_slab = a_dram.rearrange("(b t) p c s -> b p t c s", b=NBLK)
    norm_dram = nc.dram_tensor("norm_dram", (NBATCH, P, 2, BT), F32, kind="Internal").ap()
    norm_slab = norm_dram.rearrange("(h t) p k s -> h p t k s", h=NSLAB)
    cand_dram = nc.dram_tensor("cand_dram", (P, NCH, K + 1), F32, kind="Internal").ap()
    place_dram = nc.dram_tensor("place_dram", (P, NCH, K), U32, kind="Internal").ap()
    place_cells = place_dram.rearrange("p n k -> (p n k)").unsqueeze(1)

    ctx = ExitStack()
    with ctx:
        def sb(name, shape, dt=F32):
            return ctx.enter_context(nc.sbuf_tensor(name, shape, dt))

        def sem(name):
            return ctx.enter_context(nc.semaphore(name))

        b_flat = sb("b_flat", [P, max(NBLK * C * N, E * HID)])
        b_all = b_flat[:, 0:NBLK * C * N].rearrange("p (b c j) -> p b c j", b=NBLK, c=C)
        ident = sb("ident", [P, P])
        w_proj = sb("w_proj", [P, 4 * C])
        w_gate = sb("w_gate", [P, CZ])
        w_exp = sb("w_exp", [P, E])
        w_z = sb("w_z", [P, GT, CZ])

        ARENA = 19000
        arena = sb("arena", [P, ARENA])
        top = [0]

        def carve(*shape):
            n = math.prod(shape)
            v = arena[:, top[0]:top[0] + n]
            top[0] += n
            assert top[0] <= ARENA, top[0]
            names = [f"d{i}" for i in range(len(shape))]
            return v.rearrange(f"p ({' '.join(names)}) -> p {' '.join(names)}",
                               **{m: s for m, s in zip(names[1:], shape[1:])})

        x_in = carve(GU, GT, CZ)
        xT1 = carve(2, GT * P)
        half1 = carve(4, GT, 2 * C)
        prod1 = carve(4, GT, 2 * C)
        a_out = carve(2, C, BT)
        norm1 = carve(2, 4, BT)
        stdT = carve(2, BATCH, P)
        bias1 = carve(GT, 4 * C)
        st1 = carve(BT, 6)
        tmp1 = carve(6, BT)
        w_raw = carve(NW)
        bg_row = carve(CZ)
        bias_rep = carve(4 * C)
        ones_row = carve(P)
        neg_mean = carve(P)
        gw_raw = carve(CZ)
        wz_raw = carve(CZ)
        wz_bias = carve(CZ)
        wz_fold = carve(CZ)
        bz_row = carve(CZ)
        ln2_col = carve(2)
        blockmean = carve(P)
        top[0] = 0
        xq = carve(QU, QT, CZ)
        xh2 = carve(2, QT, CZ)
        xT2 = carve(2, QT * P)
        gate = carve(4, QT, CZ)
        yT = carve(QT * P)
        z = carve(C, SLAB)
        logit = carve(2 * QT, E)
        zn = carve(RT, C)
        znT = carve(RT // GT, P)
        norm_s = carve(RS, 2, RT)
        norm_r = carve(2, RT)
        a_in = carve(2, 2, N // BT, BT)
        aT_flat = carve(max(2 * NBLK * P, 2 * SLAB + RT * C))
        aT = aT_flat[:, 0:2 * NBLK * P].rearrange("p (b k i) -> p b k i", b=2, k=NBLK)
        z_mean, z_var = aT_flat[:, 0:SLAB], aT_flat[:, SLAB:2 * SLAB]
        z_sq = (zn, aT_flat[:, 2 * SLAB:2 * SLAB + RT * C].rearrange("p (s c) -> p s c", c=C))
        z_half = aT_flat[:, 2 * SLAB:3 * SLAB]
        z_scale = carve(SLAB)
        st2 = carve(QB2 * QT, 6)
        tmp2 = carve(6, QB2 * QT)
        ynorm = carve(2, QB2 * QT)
        cand = carve(QU // 2, K + 1)
        negmax = carve(QU // 2, 1)
        place = carve(QU // 2, K).bitcast(U32)
        exp_junk = carve(QT * E).bitcast(mybir.dt.bfloat16)
        top[0] = 0
        cand_all = carve(NCH, K + 1)
        cand_v = carve(NCH * K)
        w1_last = carve(HID)
        w2_last = carve(CZ)
        ex_all = carve(NCH)
        best = carve(K)
        best_at = carve(K).bitcast(U32)
        cell_f = carve(K)
        cell = carve(K).bitcast(U32)
        place_got = carve(K).bitcast(U32)
        tok_a = carve(K).bitcast(U32)
        tok_b = carve(K).bitcast(U32)
        mine = carve(2 * K + 2)
        pair = carve(2, 2 * K + 2)
        pair_v = carve(2 * K)
        top_v = carve(K)
        top_at = carve(K).bitcast(U32)
        top_at_f = carve(K)
        hot = carve(K, 2 * K)
        small = carve(8)
        send = carve(2, 2, K // 2)
        got = carve(2, K // 2)
        tok_u = carve(K // 2).bitcast(U32)
        tok_w = carve(K // 2).bitcast(U32)
        tok_wf = carve(K // 2)
        rows = carve(K // 2, CZ)
        rows_n = carve(K // 2, CZ)
        st3 = carve(K // 2, 6)
        tmp3 = carve(6, K // 2)
        norm3 = carve(2, K // 2)
        pick = carve(E)
        pooledT = carve(E)
        b1T = carve(4, E)
        hpre = carve(4, E)
        hT = carve(4, E)
        oT = carve(P)
        o_pair = carve(CZ)
        y_add = carve(K // 2, CZ)
        diag = carve(K // 2, P)
        tok_row = carve(K // 2, P)
        same = carve(K // 2, K // 2, P)
        same_before = carve(K // 2, P)
        before = carve(P)
        ones_m = carve(P)
        iota16 = carve(2 * K)
        base_col = carve(1)
        parity = carve(1).bitcast(U32)
        w_sb = b_flat[:, 0:E * HID].rearrange("p (e h) -> p e h", h=HID)
        gate_b_col = sb("gate_b_col", [P, 1])

        psum = ctx.enter_context(nc.psum_tensor("psum", [P, 8, 512], F32))

        weights_in = sem("weights_in")
        filled = sem("filled")
        setup_pe = sem("setup_pe")
        setup_dve = sem("setup_dve")
        weights_ready = sem("weights_ready")
        pool_gate = sem("pool_gate")
        act_gate = sem("act_gate")
        dve_gate = sem("dve_gate")
        sp_gate = sem("sp_gate")
        x_loaded = [sem(f"x_loaded{i}") for i in range(GU)]
        bn_done = sem("bn_done")
        norm_ready = sem("norm_ready")
        xt_psum = sem("xt_psum")
        xt_ready = sem("xt_ready")
        std_psum = sem("std_psum")
        std_ready = sem("std_ready")
        proj_ready = sem("proj_ready")
        half_ready = sem("half_ready")
        prod_ready = sem("prod_ready")
        scaled = sem("scaled")
        ab_ready = sem("ab_ready")
        a_stored = [sem(f"a_stored{i}") for i in range(2)]
        norm_stored = [sem(f"norm_stored{i}") for i in range(2)]
        xq_loaded = [sem(f"xq_loaded{i}") for i in range(QU)]
        y_stored = [sem(f"y_stored{i}") for i in range(QU)]
        a_loaded = [sem(f"a_loaded{i}") for i in range(2)]
        norm_loaded = sem("norm_loaded")
        norm_copied = sem("norm_copied")
        at_psum = sem("at_psum")
        at_ready = sem("at_ready")
        z_psum = sem("z_psum")
        z_ready = sem("z_ready")
        z_centred = sem("z_centred")
        z_squared = sem("z_squared")
        zn_ready = sem("zn_ready")
        znt_psum = sem("znt_psum")
        znt_ready = sem("znt_ready")
        xq_norm = sem("xq_norm")
        xq_psum = sem("xq_psum")
        xqt_ready = sem("xqt_ready")
        g_psum = sem("g_psum")
        gate_ready = sem("gate_ready")
        h_psum = sem("h_psum")
        gated = sem("gated")
        y_ready = sem("y_ready")
        y_psum = sem("y_psum")
        yt_ready = sem("yt_ready")
        ybn_done = sem("ybn_done")
        l_psum = sem("l_psum")
        logit_ready = sem("logit_ready")
        lt_psum = sem("lt_psum")
        cand_done = sem("cand_done")
        exp_done = sem("exp_done")
        cand_stored = sem("cand_stored")
        ends = sem("ends")
        cand_back = sem("cand_back")
        last_in = sem("last_in")
        mine_ready = sem("mine_ready")
        pair_in = sem("pair_in")
        send_ready = sem("send_ready")
        got_in = sem("got_in")
        h1_done = sem("h1_done")
        tail_pool = sem("tail_pool")
        cell_ready = sem("cell_ready")
        places_in = sem("places_in")
        tok_ready = sem("tok_ready")
        rows_in = sem("rows_in")
        final_ready = sem("final_ready")
        rows_out = sem("rows_out")
        neg_ready = sem("neg_ready")
        ex_ready = sem("ex_ready")
        hpre_ready = sem("hpre_ready")
        ht_ready = sem("ht_ready")
        diag_ready = sem("diag_ready")
        tok_row_psum = sem("tok_row_psum")
        same_ready = sem("same_ready")
        rows_ready = sem("rows_ready")
        pooled_psum = sem("pooled_psum")
        pooled_ready = sem("pooled_ready")
        b1_psum = sem("b1_psum")
        count_psum = sem("count_psum")
        o_psum = sem("o_psum")
        ot_ready = sem("ot_ready")
        yadd_ready = sem("yadd_ready")
        w1_in = [sem(f"w1_in{c}") for c in range(EC)]
        w2_in = [sem(f"w2_in{c}") for c in range(EC)]

        block = ctx.enter_context(nc.Block())

        def runs(edge, u, lag):
            return edge is None or (u >= lag if edge == "first" else u < lag)

        def rounds(eng, n, body):
            body(0, "first")
            with eng.Fori(1, n) as r:
                body(r, None)
            body(n, "last")

        def slabs(eng, fill, body):
            fill(0)
            body(0, 0, 0, "first")
            with eng.Fori(1, RS) as rr:
                body(rr, 0, rr, None)
            with eng.Fori(1, NSLAB) as h:
                fill(h)
                with eng.Fori(0, RS) as rr:
                    body(h * RS + rr, h, rr, None)
            body(NROUND, NSLAB, 0, "last")

        def z_cols(k):
            return z[:, :, k * RT:(k + 1) * RT].rearrange("p c s -> p s c")

        def group_at(n):
            return (n >> LGB) & (NBLK - 1), n & (GB - 1)

        def quad_at(n):
            return (n >> LQB) & (NBLK - 1), n & (QB - 1)

        WEIGHT_DMAS = 5 + 4 + 1 + 2 + 1 + 1 + 3 * GT

        @block.sync
        def _(sp):
            for g in range(GU):
                sp.dma_start(x_in[:, g], x_groups[0, g]).then_inc(x_loaded[g], 16)
            for i, w in enumerate((Wa1, Wb1, Wa2, Wb2)):
                sp.dma_start(w_raw[:, i * C:(i + 1) * C], w).then_inc(weights_in, 16)
            sp.dma_start(w_raw[:, 4 * C:4 * C + CZ], Wg).then_inc(weights_in, 16)
            for i, v in enumerate((ba1, bb1, ba2, bb2)):
                sp.dma_start(bias_rep[0:GT, i * C:(i + 1) * C],
                             v.unsqueeze(0).to_broadcast([GT, C])).then_inc(weights_in, 16)
            sp.dma_start(bg_row[0:1, :], bg.unsqueeze(0)).then_inc(weights_in, 16)
            for half in range(2):
                sp.dma_start(gate_b_col[half * E:(half + 1) * E, :], gate_b.unsqueeze(1)).then_inc(weights_in, 16)
            sp.dma_start(gw_raw[0:E, :], gate_w).then_inc(weights_in, 16)
            sp.dma_start(bz_row[0:1, :], bz.unsqueeze(0)).then_inc(weights_in, 16)
            for j in range(GT):
                sp.dma_start(wz_raw[j * C:(j + 1) * C, :], Wz).then_inc(weights_in, 16)
                sp.dma_start(ln2_col[j * C:(j + 1) * C, 0:1], ln2_g.unsqueeze(1)).then_inc(weights_in, 16)
                sp.dma_start(ln2_col[j * C:(j + 1) * C, 1:2], ln2_b.unsqueeze(1)).then_inc(weights_in, 16)

            with sp.Fori(1, NG // GU) as r:
                for u in range(GU):
                    n = r * GU + u
                    sp.wait_ge(xt_psum, n - GU + 1)
                    sp.wait_ge(bn_done, n - GU + 1)
                    sp.sem_inc(sp_gate, 1)
                    sp.dma_start(x_in[:, u], x_groups[group_at(n)]).then_inc(x_loaded[u], 16)
                    if u % BATCH == BATCH - 1:
                        par = u // BATCH
                        sp.wait_ge(norm_ready, r * 2 - 1 + par)
                        sp.sem_inc(sp_gate, 1)
                        sp.dma_start(norm_dram[r * 2 - 2 + par], norm1[:, par, 0:2]).then_inc(norm_stored[par], 16)
            for par in range(2):
                sp.wait_ge(norm_ready, NBATCH - 1 + par)
                sp.dma_start(norm_dram[NBATCH - 2 + par], norm1[:, par, 0:2]).then_inc(norm_stored[par], 16)

            def load_a(h, pair):
                for c in range(2):
                    sp.dma_start(a_in[:, pair % 2, c], a_slab[(h >> LSB) & (NBLK - 1), :, :, 2 * pair + c, :]
                                 ).then_inc(a_loaded[pair % 2], 16)

            sp.wait_ge(ab_ready, NG)
            for par in range(2):
                sp.wait_ge(norm_stored[par], NBATCH // 2 * 16)
                sp.wait_ge(a_stored[par], NBATCH // 2 * 16)
            load_a(0, 0)
            load_a(0, 1)

            def fill(h):
                since(sp, norm_copied, h * RS)
                sp.sem_inc(sp_gate, 1)
                sp.dma_start(norm_s, norm_slab[h]).then_inc(norm_loaded, 16)
                for pair in range(2, C // 2):
                    sp.wait_ge(at_psum, h * C + 2 * pair - 2)
                    sp.sem_inc(sp_gate, 1)
                    load_a(h, pair)
                for pair in range(2):
                    sp.wait_ge(at_psum, h * C + C - 2 + 2 * pair)
                    sp.sem_inc(sp_gate, 1)
                    load_a((h + 1) & (NSLAB - 1), pair)

            def body(r, h, rr, edge):
                for u in range(QU):
                    m = r * QU + u
                    if runs(edge, u, 7):
                        q, v = m - 7, (u - 7) % QU
                        sp.wait_ge(y_ready, q + 1)
                        sp.sem_inc(sp_gate, 1)
                        sp.dma_start(out_quads[quad_at(q)], xq[:, v]).then_inc(y_stored[v], 16)
                    if edge == "last":
                        continue
                    if edge is None:
                        sp.wait_ge(y_psum, m - QU + 1)
                        sp.wait_ge(ybn_done, m - QU + 1)
                        sp.sem_inc(sp_gate, 1)
                        sp.wait_ge(y_stored[u], r * 16)
                        sp.sem_inc(sp_gate, 1)
                    sp.dma_start(xq[:, u], x_quads[quad_at(m)]).then_inc(xq_loaded[u], 16)

            slabs(sp, fill, body)
            for u in range(QU):
                sp.wait_ge(y_stored[u], NROUND * 16)
            for i in range(2):
                sp.wait_ge(a_loaded[i], (NSLAB * C // 4 + 1) * 32)

            sp.wait_ge(cand_stored, NROUND * 32)
            sp.wait_ge(ends, 4)
            sp.dma_start(cand_all, cand_dram).then_inc(cand_back, 16)
            sp.dma_start(w1_last[0:E], weight1[:, CZ, :]).then_inc(last_in, 16)
            for half in range(2):
                sp.dma_start(w2_last[half * E:(half + 1) * E], weight2[:, HID, :]).then_inc(last_in, 16)
            for c in range(EC):
                sp.dma_start(w_sb[:, c * EG:(c + 1) * EG],
                             weight1[c * EG:(c + 1) * EG, 0:CZ, :].rearrange("e d h -> d e h")).then_inc(w1_in[c], 16)
            sp.wait_ge(mine_ready, 1)
            sp.dma_start(pair[0:E, 1], mine[E:2 * E]).then_inc(pair_in, 16)
            sp.wait_ge(send_ready, 1)
            sp.dma_start(got[E:2 * E], send[0:E, 1]).then_inc(got_in, 16)
            for c in range(EC):
                sp.wait_ge(h1_done, c + 1)
                sp.dma_start(w_sb[:, c * EG:(c + 1) * EG].rearrange("p e (g o) -> p e g o", g=4),
                             weight2[c * EG:(c + 1) * EG, 0:HID, :].rearrange("e (p g) o -> p e g o", g=4)
                             ).then_inc(w2_in[c], 16)

        @block.gpsimd
        def _(pool):
            G = nc.gpsimd
            G.memset(ident[:, :], 0.0).then_inc(filled, 1)
            G.memset(blockmean, 1.0 / C).then_inc(filled, 1)
            G.memset(ones_row, 1.0 / CZ).then_inc(filled, 1)
            G.memset(neg_mean, -1.0 / CZ).then_inc(filled, 1)
            pool.wait_ge(filled, 4)
            G.affine_select(out=ident[:, :], in_=ident[:, :], compare_op=ALU.not_equal, fill=1.0,
                            base=0, pattern=[[-1, P]], channel_multiplier=1).then_inc(filled, 1)
            bm = blockmean.rearrange("p (j c) -> p j c", c=C)
            G.affine_select(out=bm, in_=bm, compare_op=ALU.is_ge, fill=0.0, base=0,
                            pattern=[[-C, GT], [0, C]], channel_multiplier=1).then_inc(filled, 1)
            pool.wait_ge(filled, 6)
            G.affine_select(out=bm, in_=bm, compare_op=ALU.is_ge, fill=0.0, base=C - 1,
                            pattern=[[C, GT], [0, C]], channel_multiplier=-1).then_inc(filled, 1)

            with pool.Fori(0, NG // GU) as r:
                for u in range(GU):
                    par, i = u // BATCH, (u % BATCH) * GT
                    pool.wait_ge(prod_ready, r * GU + u + 1)
                    G.tensor_tensor(prod1[:, u % 4], prod1[:, u % 4],
                                    norm1[:, par, 3, i:i + GT].unsqueeze(2).to_broadcast([P, GT, 2 * C]),
                                    ALU.mult).then_inc(scaled, 1)

            pool.wait_ge(ab_ready, NG)

            def normalise_x(r, h, rr, u, m):
                if u == 0:
                    pool.wait_ge(norm_loaded, (h + 1) * 16)
                    since(pool, xq_norm, m)
                    pool.sem_inc(pool_gate, 1)
                    G.tensor_copy(norm_r, norm_s[:, rr]).then_inc(norm_copied, 1)
                    pool.wait_ge(norm_copied, r + 1)
                    pool.sem_inc(pool_gate, 1)
                pool.wait_ge(xq_loaded[u], (r + 1) * 16)
                since(pool, xq_psum, m - 1)
                pool.sem_inc(pool_gate, 1)
                for t in range(QT):
                    i = u * QT + t
                    last = G.tensor_scalar(xh2[:, u % 2, t], xq[:, u, t], norm_r[:, 0, i:i + 1],
                                           norm_r[:, 1, i:i + 1], ALU.mult, ALU.add)
                last.then_inc(xq_norm, 1)

            def body(r, h, rr, edge):
                for u in range(QU):
                    m = r * QU + u
                    if edge != "last":
                        normalise_x(r, h, rr, u, m)
                    if runs(edge, u, 3):
                        q, v = m - 3, (u - 3) % QU
                        pool.wait_ge(gated, q + 1)
                        G.tensor_tensor(xq[:, v], xq[:, v], gate[:, v % 4], ALU.add).then_inc(y_ready, 1)

            slabs(pool, lambda h: None, body)

            pool.drain()
            pool.sem_inc(ends, 1)
            pool.wait_ge(ends, 4)
            G.iota(iota16.bitcast(I32), pattern=[[1, 2 * K]], base=0, channel_multiplier=0).then_inc(tail_pool, 1)
            G.iota(base_col.bitcast(I32), pattern=[[0, 1]], base=0, channel_multiplier=NCH * K).then_inc(tail_pool, 1)
            G.memset(ones_m, 1.0).then_inc(tail_pool, 1)
            G.memset(before, 1.0).then_inc(tail_pool, 1)
            pool.wait_ge(tail_pool, 4)
            G.affine_select(out=before, in_=before, compare_op=ALU.is_gt, fill=0.0,
                            base=0, pattern=[[1, P]], channel_multiplier=-1).then_inc(tail_pool, 1)
            pool.wait_ge(cell_ready, 1)
            for k in range(K):
                pool.indirect_dma_start(out=place_got[:, k:k + 1], out_offset=None, in_=place_cells,
                                        in_offset=bass.IndirectOffsetOnAxis(ap=cell[:, k:k + 1], axis=0)
                                        ).then_inc(places_in, 16)
            pool.wait_ge(tok_ready, 1)
            for k in range(K // 2):
                pool.indirect_dma_start(out=rows[:, k], out_offset=None, in_=out_rows,
                                        in_offset=bass.IndirectOffsetOnAxis(ap=tok_u[:, k:k + 1], axis=0)
                                        ).then_inc(rows_in, 16)
            pool.wait_ge(final_ready, 1)
            for k in range(K // 2):
                pool.indirect_dma_start(out=out_rows,
                                        out_offset=bass.IndirectOffsetOnAxis(ap=tok_w[:, k:k + 1], axis=0),
                                        in_=rows[:, k], in_offset=None, bounds_check=N * N - 1, oob_is_err=False
                                        ).then_inc(rows_out, 16)
            pool.wait_ge(rows_out, 16 * K // 2)

        @block.scalar
        def _(act):
            A = nc.scalar
            def first_round(r, edge):
                for u in range(GU):
                    n = r * GU + u
                    if edge != "last":
                        if u % BATCH == 0:
                            batch = r * 2 + u // BATCH
                            act.wait_ge(std_psum, batch + 1)
                            A.activation(stdT[0:GT, u // BATCH], psum[0:GT, 7, :].rearrange("p (b q) -> p b q", b=BATCH),
                                         ACT.Copy).then_inc(std_ready, 1)
                        act.wait_ge(xt_psum, n + 1)
                        since(act, proj_ready, n - 1)
                        A.activation(xT1[:, u % 2, :], psum[:, 2 * (u % 2):2 * (u % 2) + 2, :],
                                     ACT.Copy).then_inc(xt_ready, 1)
                    if runs(edge, u, 2):
                        m, v = n - 2, (u - 2) % GU
                        act.wait_ge(proj_ready, m + 1)
                        since(act, prod_ready, m - 3)
                        pr = psum[:, 4 + v % 4, :].rearrange("p (t c) -> p t c", t=GT)
                        A.activation(half1[:, v % 4], pr[:, :, 0:2 * C], ACT.Copy).then_inc(half_ready, 1)
                    if runs(edge, u, 4):
                        m, v = n - 4, (u - 4) % GU
                        par = v // BATCH
                        act.wait_ge(scaled, m + 1)
                        if v % BATCH == 0:
                            since(act, a_stored[par], (r if u >= 4 else r - 1) * 16)
                        act.sem_inc(act_gate, 1)
                        col = (v % BATCH) * GT
                        A.activation(a_out[:, par, :, col:col + GT].rearrange("p c s -> p s c"),
                                     prod1[:, v % 4, :, 0:C], ACT.Sigmoid)
                        blk, g = group_at(m)
                        A.activation(b_all[:, blk, :, bass.ds(g * GT, GT)].rearrange("p c s -> p s c"),
                                     prod1[:, v % 4, :, C:2 * C], ACT.Sigmoid).then_inc(ab_ready, 1)
                        if v % BATCH == BATCH - 1:
                            act.wait_ge(ab_ready, m + 1)
                            act.sem_inc(act_gate, 1)
                            act.dma_start(a_dram[((m - (BATCH - 1)) >> 2) & (NBATCH - 1)],
                                          a_out[:, par]).then_inc(a_stored[par], 16)

            rounds(act, NG // GU, first_round)

            def fill(h):
                for c in range(C):
                    act.wait_ge(at_psum, h * C + c + 1)
                    since(act, z_psum, h * C + c - 1)
                    act.sem_inc(act_gate, 1)
                    A.activation(aT[:, c % 2], psum[:, c % 2, 0:NBLK * P].rearrange("p (k i) -> p k i", k=NBLK),
                                 ACT.Copy).then_inc(at_ready, 1)
                for k in range(RS):
                    act.wait_ge(z_centred, h * RS + k + 1)
                    A.activation(z_sq[k % 2], z_cols(k), ACT.Square).then_inc(z_squared, 1)

            def body(r, h, rr, edge):
                for u in range(QU):
                    n = r * QU + u
                    if edge != "last":
                        act.wait_ge(xq_psum, n + 1)
                        since(act, g_psum, n - 1)
                        A.activation(xT2[:, u % 2], psum[:, 0, :], ACT.Copy).then_inc(xqt_ready, 1)
                    if runs(edge, u, 1):
                        q, v = n - 1, (u - 1) % QU
                        act.wait_ge(g_psum, q + 1)
                        since(act, y_ready, q - 3)
                        A.activation(gate[:, v % 4], psum[:, 2 + v % 2, :].rearrange("p (t c) -> p t c", t=QT),
                                     ACT.Tanh, scale=0.5).then_inc(gate_ready, 1)
                    if u == 0 and edge != "last":
                        act.wait_ge(znt_psum, r + 1)
                        A.activation(znT, psum[:, 1, 0:RT * C].rearrange("p (g i) -> p g i", i=P),
                                     ACT.Copy, bias=1.0).then_inc(znt_ready, 1)
                    if runs(edge, u, 5):
                        q = n - 5
                        act.wait_ge(y_psum, q + 1)
                        since(act, l_psum, q)
                        A.activation(yT, psum[:, 1, :], ACT.Copy).then_inc(yt_ready, 1)
                    if u % 2 == 1 and edge != "first":
                        s, k = u // 2, (r - 1) * (QU // 2) + u // 2
                        since(act, cand_stored, (r - 1) * 32)
                        act.wait_ge(cand_done, k + 1)
                        act.sem_inc(act_gate, 1)
                        A.activation(exp_junk, psum[:, 7, :], ACT.Exp, bias=negmax[:, s],
                                     accum_out=cand[:, s, K:K + 1]).then_inc(exp_done, 1)
                        if u == QU - 1:
                            act.wait_ge(exp_done, r * (QU // 2))
                            act.sem_inc(act_gate, 1)
                            at = bass.ds((r - 1) * (QU // 2), QU // 2)
                            act.dma_start(cand_dram[:, at, :], cand).then_inc(cand_stored, 16)
                            act.dma_start(place_dram[:, at, :], place).then_inc(cand_stored, 16)

            slabs(act, fill, body)
            act.wait_ge(cand_stored, NROUND * 32)

            act.sem_inc(ends, 1)
            act.wait_ge(neg_ready, 1)
            A.activation(ex_all, cand_v.rearrange("p (n k) -> p n k", k=K)[:, :, 0], ACT.Exp, bias=mine[:, 2 * K:2 * K + 1]).then_inc(ex_ready, 1)
            act.wait_ge(neg_ready, 2)
            A.activation(small[0:E, 2:4], small[0:E, 0:2], ACT.Exp).then_inc(ex_ready, 1)
            A.activation(top_v[0:E], top_v[0:E], ACT.Exp, bias=small[0:E, 4:5]).then_inc(ex_ready, 1)
            act.wait_ge(hpre_ready, 1)
            A.activation(hT, hpre, ACT.Gelu).then_inc(ht_ready, 1)

        @block.vector
        def _(dve):
            V = nc.vector
            dve.wait_ge(weights_in, 16 * WEIGHT_DMAS)
            dve.wait_ge(filled, 7)
            V.tensor_scalar(wz_fold, wz_raw, ln2_col[:, 0:1], 0.5, ALU.mult, ALU.mult)
            V.tensor_scalar(wz_bias, wz_raw, ln2_col[:, 1:2], 0.5, ALU.mult, ALU.mult)
            V.tensor_scalar(bz_row[0:1, :], bz_row[0:1, :], CZ / (2.0 * C), None, ALU.mult)
            for t in range(GT):
                V.tensor_scalar(bias1[0:GT, t, :], bias_rep[0:GT, :], ident[0:GT, t:t + 1], None, ALU.mult)
            V.drain()
            V.tensor_tensor(wz_bias, wz_bias, wz_fold, ALU.subtract)
            dve.wait_ge(setup_pe, 1)
            V.tensor_copy(w_raw[:, 4 * C + CZ:NW], psum[:, 0, 0:E])
            V.drain().then_inc(setup_dve, 1)
            dve.wait_ge(setup_pe, 3)
            V.tensor_tensor(w_proj[:, :], w_raw[:, 0:4 * C], psum[:, 1, 0:4 * C], ALU.add)
            V.tensor_tensor(w_gate[:, :], w_raw[:, 4 * C:4 * C + CZ], psum[:, 1, 4 * C:4 * C + CZ], ALU.add)
            V.tensor_tensor(w_exp[:, :], w_raw[:, 4 * C + CZ:NW], psum[:, 1, 4 * C + CZ:NW], ALU.add)
            V.tensor_tensor(wz_fold, wz_fold, psum[:, 2, 0:CZ], ALU.add)
            V.drain()
            V.tensor_scalar(wz_fold, wz_fold, float(C), None, ALU.mult)
            V.drain()
            for j in range(GT):
                V.tensor_scalar(w_z[:, j, :], wz_fold, blockmean[:, j * C:j * C + 1], None, ALU.mult)
            V.drain().then_inc(weights_ready, 1)

            def rsqrt(v, y, t, h):
                V.tensor_scalar(h, v, -0.5, None, ALU.mult)
                V.tensor_scalar(t.bitcast(I32), v.bitcast(I32), 1, None, ALU.arith_shift_right)
                V.drain()
                V.tensor_scalar(y.bitcast(I32), t.bitcast(I32), -1.0, float(RSQRT_MAGIC), ALU.mult, ALU.add)
                for _ in range(3):
                    V.drain()
                    V.tensor_tensor(t, y, y, ALU.mult)
                    V.drain()
                    V.tensor_tensor(t, t, h, ALU.mult)
                    V.drain()
                    V.scalar_tensor_tensor(y, t, 1.5, y, ALU.add, ALU.mult)
                V.drain()

            def scales(st, tmp, scale, eps):
                even, odd = st[:, :, 1], st[:, :, 4]
                V.drain()
                V.tensor_tensor(tmp[:, 1], even, odd, ALU.subtract)
                V.tensor_tensor(tmp[:, 2], st[:, :, 2], st[:, :, 5], ALU.add)
                V.tensor_tensor(tmp[:, 0], even, odd, ALU.add)
                V.drain()
                V.scalar_tensor_tensor(tmp[:, 1], tmp[:, 1], CZ / 4.0, tmp[:, 1], ALU.mult, ALU.mult)
                V.drain()
                V.tensor_tensor(tmp[:, 2], tmp[:, 2], tmp[:, 1], ALU.add)
                V.drain()
                V.tensor_scalar(tmp[:, 1], tmp[:, 2], 1.0 / CZ, eps, ALU.mult, ALU.add)
                V.drain()
                rsqrt(tmp[:, 1], scale, tmp[:, 3], tmp[:, 4])

            def first_round(r, edge):
                for u in range(GU):
                    n = r * GU + u
                    par = u // BATCH
                    if edge != "last":
                        dve.wait_ge(x_loaded[u], (r + 1) * 16)
                        for t in range(GT):
                            last = V.bn_stats(st1[:, (u % BATCH) * GT + t], x_in[:, u, t])
                        last.then_inc(bn_done, 1)
                    if runs(edge, u, 8):
                        m, v = n - 8, u
                        dve.wait_ge(half_ready, m + 1)
                        since(dve, ab_ready, m - min(u, 3))
                        pr = psum[:, 4 + v % 4, :].rearrange("p (t c) -> p t c", t=GT)
                        V.tensor_tensor(prod1[:, v % 4], half1[:, v % 4], pr[:, :, 2 * C:4 * C],
                                        ALU.mult).then_inc(prod_ready, 1)
                    if u % BATCH == BATCH - 1 and edge != "last":
                        since(dve, norm_stored[par], r * 16)
                        since(dve, scaled, n - GU + 1)
                        dve.sem_inc(dve_gate, 1)
                        scale, shift, std, scale2 = (norm1[:, par, i] for i in range(4))
                        scales(st1, tmp1, scale, EPS_C)
                        V.tensor_tensor(std, tmp1[:, 1], scale, ALU.mult)
                        V.tensor_tensor(scale2, scale, scale, ALU.mult)
                        V.scalar_tensor_tensor(tmp1[:, 5], tmp1[:, 0], -0.5, scale, ALU.mult, ALU.mult)
                        V.drain()
                        V.tensor_scalar(shift, tmp1[:, 5], 1.0, None, ALU.add).then_inc(norm_ready, 1)

            rounds(dve, NG // GU, first_round)

            dve.wait_ge(ab_ready, NG)

            def fill(h):
                for c in range(C):
                    dve.wait_ge(z_psum, h * C + c + 1)
                    V.tensor_copy(z[:, c, :], psum[:, 2 + c % 2, 0:SLAB]).then_inc(z_ready, 1)
                V.drain()
                V.tensor_reduce(out=z_mean, in_=z.rearrange("p c s -> p s c"), op=ALU.add, axis=AX.X)
                V.drain()
                for k in range(RS + 1):
                    if k < RS:
                        V.scalar_tensor_tensor(z_cols(k), z_mean[:, k * RT:(k + 1) * RT].unsqueeze(2).to_broadcast([P, RT, C]),
                                               -1.0 / C, z_cols(k), ALU.mult, ALU.add).then_inc(z_centred, 1)
                    if k >= 1:
                        dve.wait_ge(z_squared, h * RS + k)
                        V.tensor_reduce(out=z_var[:, (k - 1) * RT:k * RT], in_=z_sq[(k - 1) % 2], op=ALU.add, axis=AX.X)
                V.drain()
                V.tensor_scalar(z_var, z_var, 1.0 / C, EPS_T, ALU.mult, ALU.add)
                V.drain()
                rsqrt(z_var, z_scale, z_mean, z_half)

            def body(r, h, rr, edge):
                for u in range(QU):
                    n = r * QU + u
                    if u == 0 and edge != "last":
                        since(dve, znt_psum, r)
                        at = bass.ds(rr * RT, RT)
                        V.tensor_tensor(zn, z[:, :, at].rearrange("p c s -> p s c"),
                                        z_scale[:, at].unsqueeze(2).to_broadcast([P, RT, C]),
                                        ALU.mult).then_inc(zn_ready, 1)
                    if u % 2 == 0 and edge != "first":
                        k = (r - 1) * (QU // 2) + u // 2
                        dve.wait_ge(l_psum, n - 6)
                        since(dve, lt_psum, k)
                        scale = ynorm[:, u // 4, (u // 2 % 2) * 2 * QT:(u // 2 % 2 + 1) * 2 * QT]
                        V.tensor_tensor(logit, psum[:, 6, :].rearrange("p (t e) -> p t e", e=E),
                                        scale.unsqueeze(2).to_broadcast([P, 2 * QT, E]),
                                        ALU.mult).then_inc(logit_ready, 1)
                    if runs(edge, u, 2):
                        q, v = n - 2, (u - 2) % QU
                        dve.wait_ge(gate_ready, q + 1)
                        dve.wait_ge(h_psum, q + 1)
                        V.scalar_tensor_tensor(gate[:, v % 4], gate[:, v % 4], 1.0,
                                               psum[:, 4 + v % 2, :].rearrange("p (t c) -> p t c", t=QT),
                                               ALU.add, ALU.mult).then_inc(gated, 1)
                    if runs(edge, u, 4):
                        q, v = n - 4, (u - 4) % QU
                        dve.wait_ge(y_ready, q + 1)
                        for t in range(QT):
                            last = V.bn_stats(st2[:, v % QB2 * QT + t], xq[:, v, t])
                        last.then_inc(ybn_done, 1)
                        if v % QB2 == QB2 - 1:
                            scales(st2, tmp2, ynorm[:, v // QB2], EPS_T)
                    if u % 2 == 1 and edge != "first":
                        s, k = u // 2, (r - 1) * (QU // 2) + u // 2
                        dve.wait_ge(lt_psum, k + 1)
                        since(dve, cand_stored, (r - 1) * 32)
                        dve.sem_inc(dve_gate, 1)
                        V.max(out=cand[:, s, 0:K], in_=psum[:, 7, :])
                        V.drain()
                        V.tensor_scalar(negmax[:, s], cand[:, s, 0:1], -1.0, None, ALU.mult)
                        V.max_index(out=place[:, s], in_max=cand[:, s, 0:K], in_values=psum[:, 7, :])
                        V.drain().then_inc(cand_done, 1)

            slabs(dve, fill, body)

            V.drain().then_inc(ends, 1)
            dve.wait_ge(tail_pool, 5)
            dve.wait_ge(cand_back, 16)
            V.tensor_copy(iota16, iota16.bitcast(I32))
            V.tensor_copy(base_col, base_col.bitcast(I32))
            V.memset(parity, 0)
            V.tensor_tensor(pick, ident[:, 0:E], ident[:, E:2 * E], ALU.add)
            V.tensor_scalar(cand_v.rearrange("p (n k) -> p n k", k=K), cand_all[:, :, 0:K], gate_b_col[:, :], None, ALU.add)
            V.drain()
            V.max(out=best, in_=cand_v)
            V.drain()
            V.memset(parity[E:2 * E], 1)
            V.max_index(out=best_at, in_max=best, in_values=cand_v)
            V.tensor_copy(mine[:, 0:K], best)
            V.tensor_scalar(mine[:, 2 * K:2 * K + 1], best[:, 0:1], -1.0, None, ALU.mult).then_inc(neg_ready, 1)
            V.drain()
            V.tensor_copy(cell_f, best_at)
            V.drain()
            V.tensor_scalar(cell_f, cell_f, base_col, None, ALU.add)
            V.drain()
            V.tensor_copy(cell, cell_f)
            V.drain().then_inc(cell_ready, 1)
            dve.wait_ge(ex_ready, 1)
            V.tensor_tensor(ex_all, ex_all, cand_all[:, :, K], ALU.mult)
            V.drain()
            V.tensor_reduce(out=mine[:, 2 * K + 1:2 * K + 2], in_=ex_all, op=ALU.add, axis=AX.X)
            V.tensor_scalar(tok_a, best_at, LN, LN + 7, ALU.logical_shift_right, ALU.logical_shift_left)
            V.tensor_scalar(tok_b, best_at, N - GT, None, ALU.bitwise_and)
            V.drain()
            V.tensor_tensor(tok_a, tok_a, tok_b, ALU.bitwise_or)
            dve.wait_ge(places_in, 16 * K)
            V.drain()
            V.tensor_scalar(tok_b, place_got, P - 1, LN, ALU.bitwise_and, ALU.logical_shift_left)
            V.drain()
            V.tensor_tensor(tok_a, tok_a, tok_b, ALU.bitwise_or)
            V.drain()
            V.tensor_scalar(tok_b, place_got, 7, 1, ALU.logical_shift_right, ALU.logical_shift_left)
            V.drain()
            V.tensor_tensor(tok_a, tok_a, tok_b, ALU.bitwise_or)
            V.drain()
            V.tensor_tensor(tok_a, tok_a, parity.to_broadcast([P, K]), ALU.bitwise_or)
            V.drain()
            V.tensor_copy(mine[:, K:2 * K], tok_a)
            V.drain().then_inc(mine_ready, 1)
            dve.wait_ge(pair_in, 16)
            V.tensor_copy(pair[0:E, 0], mine[0:E])
            V.drain()
            V.tensor_copy(pair_v[0:E].rearrange("p (a k) -> p a k", a=2), pair[0:E, :, 0:K])
            V.drain()
            V.max(out=top_v[0:E], in_=pair_v[0:E])
            V.drain()
            V.max_index(out=top_at[0:E], in_max=top_v[0:E], in_values=pair_v[0:E])
            V.tensor_scalar(small[0:E, 4:5], top_v[0:E, 0:1], -1.0, None, ALU.mult)
            V.drain()
            V.tensor_copy(top_at_f[0:E], top_at[0:E])
            V.scalar_tensor_tensor(small[0:E, 0:2], pair[0:E, :, 2 * K], -1.0,
                                   small[0:E, 4:5].to_broadcast([E, 2]), ALU.mult, ALU.add)
            V.drain().then_inc(neg_ready, 1)
            V.tensor_tensor(hot[0:E], iota16[0:E].unsqueeze(1).to_broadcast([E, K, 2 * K]),
                            top_at_f[0:E].unsqueeze(2).to_broadcast([E, K, 2 * K]), ALU.is_equal)
            V.drain()
            for a in range(2):
                V.tensor_tensor(hot[0:E, :, a * K:(a + 1) * K], hot[0:E, :, a * K:(a + 1) * K],
                                pair[0:E, a, K:2 * K].unsqueeze(1).to_broadcast([E, K, K]), ALU.mult)
            dve.wait_ge(ex_ready, 3)
            V.drain()
            V.tensor_reduce(out=send[0:E, :, 0].rearrange("p a k -> p k a"),
                            in_=hot[0:E].rearrange("p (k a) m -> p k a m", a=2), op=ALU.add, axis=AX.X)
            V.tensor_tensor(small[0:E, 2:4], small[0:E, 2:4], pair[0:E, :, 2 * K + 1], ALU.mult)
            V.drain()
            V.tensor_tensor(small[0:E, 5:6], small[0:E, 2:3], small[0:E, 3:4], ALU.add)
            V.drain()
            V.reciprocal(small[0:E, 6:7], small[0:E, 5:6])
            V.drain()
            V.tensor_scalar(send[0:E, :, 1].rearrange("p a k -> p k a"),
                            top_v[0:E].rearrange("p (k a) -> p k a", a=2), small[0:E, 6:7], None, ALU.mult)
            V.drain()
            V.tensor_copy(got[0:E], send[0:E, 0])
            V.drain().then_inc(send_ready, 1)
            dve.wait_ge(got_in, 16)
            V.tensor_copy(tok_u, got[:, 0])
            V.drain().then_inc(tok_ready, 1)
            for k in range(K // 2):
                V.tensor_scalar(diag[:, k], ident[:, :], got[:, 0, k:k + 1], None, ALU.mult)
            V.drain().then_inc(diag_ready, 1)
            dve.wait_ge(tok_row_psum, 1)
            V.tensor_copy(tok_row, psum[:, 0, :].rearrange("p (k q) -> p k q", q=P))
            V.drain()
            for s in range(K // 2):
                for t in range(K // 2):
                    V.tensor_scalar(same[:, s, t], tok_row[:, t], got[:, 0, s:s + 1], None, ALU.is_equal)
            V.drain()
            for t in range(K // 2):
                V.tensor_tensor(same_before[:, t], same[:, t, t], before, ALU.mult)
            V.drain().then_inc(same_ready, 1)
            dve.wait_ge(rows_in, 16 * K // 2)
            for k in range(K // 2):
                V.bn_stats(st3[:, k], rows[:, k])
            scales(st3, tmp3, norm3[:, 0], EPS_T)
            V.scalar_tensor_tensor(norm3[:, 1], tmp3[:, 0], -0.5, norm3[:, 0], ALU.mult, ALU.mult)
            V.drain()
            for k in range(K // 2):
                V.tensor_scalar(rows_n[:, k], rows[:, k], norm3[:, 0, k:k + 1], norm3[:, 1, k:k + 1], ALU.mult, ALU.add)
            V.drain()
            for k in range(K // 2):
                V.tensor_scalar(rows_n[:, k], rows_n[:, k], got[:, 1, k:k + 1], None, ALU.mult)
            V.drain().then_inc(rows_ready, 1)
            dve.wait_ge(pooled_psum, 1)
            V.tensor_copy(pooledT, psum[:, 1, 0:E])
            V.drain().then_inc(pooled_ready, 1)
            dve.wait_ge(b1_psum, 1)
            V.tensor_copy(b1T, psum[:, 2, 0:4 * E].rearrange("p (g e) -> p g e", g=4))
            dve.wait_ge(count_psum, 1)
            V.tensor_scalar(tok_wf, psum[:, 5, 0:K // 2], 1.0, float(2 * N * N), ALU.min, ALU.mult)
            V.drain()
            V.tensor_tensor(tok_wf, tok_wf, got[:, 0], ALU.add)
            V.drain()
            V.tensor_copy(tok_w, tok_wf)
            dve.wait_ge(h1_done, EC)
            V.tensor_tensor(hpre, b1T, psum[:, 3, 0:4 * E].rearrange("p (g e) -> p g e", g=4), ALU.add)
            V.drain().then_inc(hpre_ready, 1)
            dve.wait_ge(o_psum, 1)
            for half in range(2):
                V.tensor_copy(oT[:, half * E:(half + 1) * E], psum[:, 4, 0:E])
            V.drain().then_inc(ot_ready, 1)
            dve.wait_ge(o_psum, 2)
            dve.wait_ge(last_in, 48)
            V.tensor_tensor(o_pair, w2_last, psum[:, 6, 0:CZ], ALU.add)
            V.drain()
            for k in range(K // 2):
                V.tensor_scalar(y_add[:, k], o_pair, got[:, 1, k:k + 1], None, ALU.mult)
            V.drain().then_inc(yadd_ready, 1)
            dve.wait_ge(o_psum, 3)
            V.tensor_tensor(rows, rows, psum[:, 7, :].rearrange("p (k c) -> p k c", c=CZ), ALU.add)
            V.drain().then_inc(final_ready, 1)

        @block.tensor
        def _(pe):
            PE = nc.tensor
            pe.wait_ge(weights_in, 16 * WEIGHT_DMAS)
            pe.wait_ge(filled, 7)
            PE.transpose(psum[:, 0, 0:E], gw_raw[0:E, :], ident[0:E, 0:E]).then_inc(setup_pe, 1)
            pe.wait_ge(setup_dve, 1)
            PE.matmul(psum[:, 1, 0:NW], neg_mean, w_raw, start=True, stop=False)
            PE.matmul(psum[:, 1, 4 * C:4 * C + CZ], ones_row[0:1, :], bg_row[0:1, :],
                      start=False, stop=True).then_inc(setup_pe, 1)
            PE.matmul(psum[:, 2, 0:CZ], blockmean, wz_bias, start=True, stop=False)
            PE.matmul(psum[:, 2, 0:CZ], ones_row[0:1, :], bz_row[0:1, :], start=False, stop=True).then_inc(setup_pe, 1)
            pe.wait_ge(weights_ready, 1)

            def first_round(r, edge):
                for u in range(GU):
                    n = r * GU + u
                    if u % BATCH == 0 and edge != "last":
                        par = u // BATCH
                        pe.wait_ge(norm_ready, r * 2 + par + 1)
                        since(pe, prod_ready, n - 4)
                        for g in range(BATCH):
                            last = PE.transpose(psum[0:GT, 7, g * P:(g + 1) * P],
                                                norm1[:, par, 2, g * GT:(g + 1) * GT], ident[:, :])
                        last.then_inc(std_psum, 1)
                    loads, projects = edge != "last", runs(edge, u, 2)
                    m, v = n - 2, (u - 2) % GU
                    if loads:
                        pe.wait_ge(x_loaded[u], (r + 1) * 16)
                        since(pe, xt_ready, n - 1)
                    if projects:
                        pe.wait_ge(xt_ready, m + 1)
                        since(pe, prod_ready, m - 3)
                        pe.wait_ge(std_ready, r * 2 + ((u - 1) // BATCH + 1 if loads else 0))
                        PE.matmul(psum[:, 4 + v % 4, :], stdT[0:GT, v // BATCH, v % BATCH], bias1[0:GT].rearrange("p t c -> p (t c)"),
                                  start=True, stop=False)
                    for t in range(GT):
                        if loads:
                            xt = PE.transpose(psum[:, 2 * (u % 2) + t // 4, (t % 4) * P:(t % 4 + 1) * P],
                                              x_in[:, u, t], ident[:, :])
                        if projects:
                            pr = PE.matmul(psum[:, 4 + v % 4, t * 4 * C:(t + 1) * 4 * C],
                                           xT1[:, v % 2, t * P:(t + 1) * P], w_proj[:, :],
                                           start=False, stop=(t == GT - 1))
                    if loads:
                        xt.then_inc(xt_psum, 1)
                    if projects:
                        pr.then_inc(proj_ready, 1)

            rounds(pe, NG // GU, first_round)

            pe.wait_ge(ab_ready, NG)

            def fill(h):
                since(pe, xqt_ready, h * QS)
                since(pe, yt_ready, h * QS - 5)
                since(pe, gate_ready, h * QS - 1)
                for c in range(C + 1):
                    if c < C:
                        pe.wait_ge(a_loaded[c // 2 % 2], (h * (C // 4) + c // 4 + 1) * 32)
                        since(pe, at_ready, h * C + c - 1)
                        for k in range(NBLK):
                            last = PE.transpose(psum[:, c % 2, k * P:(k + 1) * P],
                                                a_in[:, c // 2 % 2, c % 2, k * (P // BT):(k + 1) * (P // BT)].rearrange("p t s -> p (t s)"),
                                                ident[:, :])
                        last.then_inc(at_psum, 1)
                    if c >= 1:
                        pe.wait_ge(at_ready, h * C + c)
                        since(pe, z_ready, h * C + c - 2)
                        for k in range(NBLK):
                            last = PE.matmul(psum[:, 2 + (c - 1) % 2, 0:SLAB], aT[:, (c - 1) % 2, k],
                                             b_all[:, k, c - 1, bass.ds((h & (SB - 1)) * SLAB, SLAB)],
                                             start=(k == 0), stop=(k == NBLK - 1))
                        last.then_inc(z_psum, 1)

            def body(r, h, rr, edge):
                for u in range(QU):
                    n = r * QU + u
                    if u % 2 == 1 and edge != "first":
                        k = (r - 1) * (QU // 2) + u // 2
                        pe.wait_ge(logit_ready, k + 1)
                        since(pe, exp_done, k)
                        since(pe, cand_done, k)
                        for g in range(QT):
                            last = PE.transpose(psum[:, 7, g * P:(g + 1) * P],
                                                logit[:, 2 * g:2 * g + 2, :].rearrange("p t e -> p (t e)"), ident[:, :])
                        last.then_inc(lt_psum, 1)
                    if edge != "last":
                        pe.wait_ge(xq_norm, n + 1)
                        since(pe, xqt_ready, n)
                        for t in range(QT):
                            last = PE.transpose(psum[:, 0, t * P:(t + 1) * P], xh2[:, u % 2, t], ident[:, :])
                        last.then_inc(xq_psum, 1)
                    if runs(edge, u, 1):
                        q, v = n - 1, (u - 1) % QU
                        if u == 0 and edge is None:
                            pe.wait_ge(z_ready, (h + 1) * C)
                        if u == 1 and edge == "first":
                            pe.wait_ge(z_ready, C)
                        pe.wait_ge(xqt_ready, q + 1)
                        since(pe, gate_ready, q - 1)
                        for t in range(QT):
                            last = PE.matmul(psum[:, 2 + v % 2, t * CZ:(t + 1) * CZ], xT2[:, v % 2, t * P:(t + 1) * P],
                                             w_gate[:, :], start=True, stop=True)
                        last.then_inc(g_psum, 1)
                        if u == 1:
                            pe.wait_ge(znt_ready, r + 1)
                        since(pe, gated, q - 1)
                        PE.matmul(psum[:, 4 + v % 2, :], znT[:, v // 2],
                                  w_z[:, (v % 2) * QT:(v % 2 + 1) * QT, :].rearrange("p t c -> p (t c)"),
                                  start=True, stop=True).then_inc(h_psum, 1)
                    if u == 0 and edge != "last":
                        pe.wait_ge(zn_ready, r + 1)
                        if edge is None:
                            pe.wait_ge(yt_ready, n - 5)
                        for g in range(RT // GT):
                            last = PE.transpose(psum[:, 1, g * P:(g + 1) * P],
                                                zn[:, g * GT:(g + 1) * GT, :].rearrange("p s c -> p (s c)"), ident[:, :])
                        last.then_inc(znt_psum, 1)
                    if runs(edge, u, 6):
                        q, v = n - 6, (u - 6) % QU
                        pe.wait_ge(yt_ready, q + 1)
                        if v % 2 == 0:
                            since(pe, logit_ready, (r * QU + u - 6) >> 1)
                        for t in range(QT):
                            last = PE.matmul(psum[:, 6, (v % 2 * QT + t) * E:(v % 2 * QT + t + 1) * E],
                                             yT[:, t * P:(t + 1) * P], w_exp[:, :], start=True, stop=True)
                        last.then_inc(l_psum, 1)
                    if runs(edge, u, 5):
                        q, v = n - 5, (u - 5) % QU
                        pe.wait_ge(y_ready, q + 1)
                        since(pe, yt_ready, q)
                        if u == 0 and edge != "last":
                            pe.wait_ge(znt_ready, r + 1)
                        for t in range(QT):
                            last = PE.transpose(psum[:, 1, t * P:(t + 1) * P], xq[:, v, t], ident[:, :])
                        last.then_inc(y_psum, 1)

            slabs(pe, fill, body)

            pe.drain()
            pe.sem_inc(ends, 1)
            pe.wait_ge(diag_ready, 1)
            pe.wait_ge(tail_pool, 5)
            for k in range(K // 2):
                last = PE.matmul(psum[:, 0, k * P:(k + 1) * P], ones_m, diag[:, k], start=True, stop=True)
            last.then_inc(tok_row_psum, 1)
            pe.wait_ge(last_in, 48)
            for g in range(4):
                last = PE.transpose(psum[:, 2, g * E:(g + 1) * E], w1_last[0:E, bass.ds(g, P, 4)], ident[0:E, 0:E])
            last.then_inc(b1_psum, 1)
            pe.wait_ge(same_ready, 1)
            for t in range(K // 2):
                for s in range(t + 1):
                    last = PE.matmul(psum[:, 5, t:t + 1], same[:, s, t] if s < t else same_before[:, t],
                                     ones_m[:, 0:1], start=(s == 0), stop=(s == t))
            last.then_inc(count_psum, 1)
            pe.wait_ge(rows_ready, 1)
            for k in range(K // 2):
                last = PE.matmul(psum[:, 1, 0:E], rows_n[:, k], pick, start=(k == 0), stop=(k == K // 2 - 1))
            last.then_inc(pooled_psum, 1)
            pe.wait_ge(pooled_ready, 1)
            for c in range(EC):
                pe.wait_ge(w1_in[c], 16)
                for e in range(c * EG, (c + 1) * EG):
                    for g in range(4):
                        last = PE.matmul(psum[:, 3, g * E + e:g * E + e + 1], w_sb[:, e, bass.ds(g, P, 4)],
                                         pooledT[:, e:e + 1], start=True, stop=True)
                last.then_inc(h1_done, 1)
            pe.wait_ge(ht_ready, 1)
            for c in range(EC):
                pe.wait_ge(w2_in[c], 16)
                for e in range(c * EG, (c + 1) * EG):
                    for g in range(4):
                        last = PE.matmul(psum[:, 4, e:e + 1], w_sb[:, e, g * CZ:(g + 1) * CZ], hT[:, g, e:e + 1],
                                         start=(g == 0), stop=(g == 3))
            last.then_inc(o_psum, 1)
            pe.wait_ge(ot_ready, 1)
            PE.transpose(psum[:, 6, 0:CZ], oT, ident[:, :]).then_inc(o_psum, 1)
            pe.wait_ge(yadd_ready, 1)
            for t in range(K // 2):
                for s in range(K // 2):
                    last = PE.matmul(psum[:, 7, t * CZ:(t + 1) * CZ], same[:, s, t], y_add[:, s],
                                     start=(s == 0), stop=(s == K // 2 - 1))
            last.then_inc(o_psum, 1)


_INS = ["x", "L0_conv_Wa1", "L0_conv_ba1", "L0_conv_Wa2", "L0_conv_ba2", "L0_conv_Wb1", "L0_conv_bb1",
        "L0_conv_Wb2", "L0_conv_bb2", "L0_conv_ln2_g", "L0_conv_ln2_b", "L0_conv_Wg", "L0_conv_bg",
        "L0_conv_Wz", "L0_conv_bz", "L0_ffn_gate_w", "L0_ffn_gate_b", "L0_ffn_weight1", "L0_ffn_weight2"]


def kernel(**inputs):
    import numpy as _np
    import concourse.bacc as _bacc
    from concourse import mybir as _mybir
    from concourse.bass_utils import run_bass_kernel_spmd as _run

    nc = _bacc.Bacc("TRN2", target_bir_lowering=False, num_devices=1)
    arrays, args = {}, []
    for name in _INS:
        a = _np.ascontiguousarray(inputs[name])
        arrays[f"in_{name}_dram"] = a
        args.append(nc.dram_tensor(f"in_{name}_dram", a.shape, _mybir.dt.from_np(a.dtype), kind="ExternalInput").ap())
    shape = inputs["x"].shape
    args.append(nc.dram_tensor("out_0_dram", shape, _mybir.dt.from_np(_np.dtype("float32")), kind="ExternalOutput").ap())
    build(nc, *args)
    r = _run(nc, [arrays], core_ids=[0])
    return r.results[0]["out_0_dram"]
```

```python
import math
from contextlib import ExitStack

import concourse.bass as bass
from concourse import mybir

F32 = mybir.dt.float32
I32 = mybir.dt.int32
U32 = mybir.dt.uint32
ALU = mybir.AluOpType
ACT = mybir.ActivationFunctionType
AX = mybir.AxisListType

P = 128
CZ = 128
C = 16
E = 64
HID = 512
K = 8
EPS_C = 1e-6
EPS_T = 1e-5
RSQRT_MAGIC = 0x5F3759DF
ROOT_CZ = math.sqrt(CZ)

GT = 8
GU = 8
BATCH = 4
BT = BATCH * GT

QT = 4
QU = 8
RT = QU * QT
QB2 = 4
SLAB = 256


def since(eng, sem, value):
    if not (isinstance(value, int) and value <= 0):
        eng.wait_ge(sem, value)


def build(nc, x, Wa1, ba1, Wa2, ba2, Wb1, bb1, Wb2, bb2, ln2_g, ln2_b, Wg, bg, Wz, bz,
          gate_w, gate_b, weight1, weight2, out):
    N = x.shape[1]
    LN = N.bit_length() - 1
    NBLK = N // P
    GB = N // GT
    NG = NBLK * GB
    LGB = GB.bit_length() - 1
    NQ = NG * GT // QT
    QB = N // QT
    LQB = QB.bit_length() - 1
    NSLAB = NBLK * (N // SLAB)
    SB = N // SLAB
    LSB = SB.bit_length() - 1
    QS = SLAB // QT
    RS = QS // QU
    NROUND = NQ // QU
    NBATCH = NG // BATCH
    NW = 4 * C + CZ + E
    EG = 8
    EC = E // EG
    NCH = NG

    x_groups = x[0].rearrange("(b p) (g s) c -> b g p s c", p=P, s=GT)
    x_quads = x[0].rearrange("(b p) (g s) c -> b g p s c", p=P, s=QT)
    out_quads = out[0].rearrange("(b p) (g s) c -> b g p s c", p=P, s=QT)
    out_rows = out[0].rearrange("i j c -> (i j) c")

    a_dram = nc.dram_tensor("a_dram", (NBATCH, P, C, BT), F32, kind="Internal").ap()
    a_slab = a_dram.rearrange("(b t) p c s -> b p t c s", b=NBLK)
    norm_dram = nc.dram_tensor("norm_dram", (NBATCH, P, 2, BT), F32, kind="Internal").ap()
    norm_slab = norm_dram.rearrange("(h t) p k s -> h p t k s", h=NSLAB)
    cand_dram = nc.dram_tensor("cand_dram", (P, NCH, K + 1), F32, kind="Internal").ap()
    place_dram = nc.dram_tensor("place_dram", (P, NCH, K), U32, kind="Internal").ap()
    place_cells = place_dram.rearrange("p n k -> (p n k)").unsqueeze(1)

    ctx = ExitStack()
    with ctx:
        def sb(name, shape, dt=F32):
            return ctx.enter_context(nc.sbuf_tensor(name, shape, dt))

        def sem(name):
            return ctx.enter_context(nc.semaphore(name))

        b_flat = sb("b_flat", [P, max(NBLK * C * N, E * HID)])
        b_all = b_flat[:, 0:NBLK * C * N].rearrange("p (b c j) -> p b c j", b=NBLK, c=C)
        ident = sb("ident", [P, P])
        w_proj = sb("w_proj", [P, 4 * C])
        w_gate = sb("w_gate", [P, CZ])
        w_exp = sb("w_exp", [P, E])
        w_z = sb("w_z", [P, GT, CZ])

        ARENA = 19016
        arena = sb("arena", [P, ARENA])
        top = [0]

        def carve(*shape):
            n = math.prod(shape)
            v = arena[:, top[0]:top[0] + n]
            top[0] += n
            assert top[0] <= ARENA, top[0]
            names = [f"d{i}" for i in range(len(shape))]
            return v.rearrange(f"p ({' '.join(names)}) -> p {' '.join(names)}",
                               **{m: s for m, s in zip(names[1:], shape[1:])})

        x_in = carve(GU, GT, CZ)
        xT1 = carve(2, GT * P)
        proj1 = carve(4, GT, 4 * C)
        prod1 = carve(4, GT, 2 * C)
        a_out = carve(2, C, BT)
        norm1 = carve(2, 4, BT)
        stdT = carve(2, BATCH, P)
        bias1 = carve(GT, 4 * C)
        st1 = carve(BT, 6)
        tmp1 = carve(6, BT)
        w_raw = carve(NW)
        bg_row = carve(CZ)
        bias_rep = carve(4 * C)
        ones_row = carve(P)
        neg_mean = carve(P)
        gw_raw = carve(CZ)
        wz_raw = carve(CZ)
        wz_bias = carve(CZ)
        wz_fold = carve(CZ)
        bz_row = carve(CZ)
        ln2_col = carve(2)
        blockmean = carve(P)
        top[0] = 0
        xq = carve(QU, QT, CZ)
        xh2 = carve(2, QT, CZ)
        xT2 = carve(2, QT * P)
        gate = carve(4, QT, CZ)
        yT = carve(QT * P)
        z = carve(C, SLAB)
        logit = carve(2 * QT, E)
        zn = carve(RT, C)
        znT = carve(RT // GT, P)
        norm_s = carve(RS, 2, RT)
        norm_r = carve(2, RT)
        a_in = carve(2, 2, N // BT, BT)
        aT = carve(2, NBLK, P)
        z_sum = carve(SLAB)
        z_scale = carve(SLAB)
        z_var = carve(SLAB)
        z_sq = [zn[:, i * RT // 2:(i + 1) * RT // 2].rearrange("p s c -> p (s c)") for i in range(2)]
        z_tmp = z_sq[0]
        st2 = carve(QB2 * QT, 6)
        tmp2 = carve(4, QB2 * QT)
        yroot = carve(2, QB2 * QT)
        cand = carve(QU // 2, K + 1)
        negmax = carve(QU // 2, 1)
        place = carve(QU // 2, K).bitcast(U32)
        top[0] = 0
        early = carve(max(NCH * (2 * K + 1), (K // 2) * (K // 2 + 2) * P))
        cand_all = early[:, 0:NCH * (K + 1)].rearrange("p (n k) -> p n k", k=K + 1)
        cand_v = early[:, NCH * (K + 1):NCH * (2 * K + 1)]
        w1_last = carve(HID)
        w2_last = carve(CZ)
        ex_all = carve(NCH)
        best = carve(K)
        best_at = carve(K).bitcast(U32)
        cell_f = carve(K)
        cell = carve(K).bitcast(U32)
        place_got = carve(K).bitcast(U32)
        tok_a = carve(K).bitcast(U32)
        tok_b = carve(K).bitcast(U32)
        mine = carve(2 * K + 2)
        pair = carve(2, 2 * K + 2)
        pair_v = carve(2 * K)
        top_v = carve(K)
        top_at = carve(K).bitcast(U32)
        top_at_f = carve(K)
        hot = carve(K, 2 * K)
        small = carve(8)
        send = carve(2, 2, K // 2)
        got = carve(2, K // 2)
        tok_u = carve(K // 2).bitcast(U32)
        tok_w = carve(K // 2).bitcast(U32)
        tok_wf = carve(K // 2)
        rows = carve(K // 2, CZ)
        rows_n = carve(K // 2, CZ)
        st3 = carve(K // 2, 6)
        tmp3 = carve(6, K // 2)
        norm3 = carve(2, K // 2)
        pick = carve(E)
        pooled1 = carve(2, 32 * 32)
        hidden4 = carve(4, 2, 32 * 32)
        hpre = carve(HID)
        hid = hpre
        o_sb = carve(CZ)
        twice = carve(P)
        o_pair = carve(CZ)
        y_add = carve(K // 2, CZ)
        diag = y_add
        same = early[:, 0:(K // 2) ** 2 * P].rearrange("p (s t q) -> p s t q", t=K // 2, q=P)
        same_before = early[:, (K // 2) ** 2 * P:(K // 2) * (K // 2 + 1) * P].rearrange("p (t q) -> p t q", q=P)
        tok_row = early[:, (K // 2) * (K // 2 + 1) * P:(K // 2) * (K // 2 + 2) * P].rearrange("p (t q) -> p t q", q=P)
        before = carve(P)
        ones_m = carve(P)
        iota16 = carve(2 * K)
        base_col = carve(1)
        parity = carve(1).bitcast(U32)
        w_sb = b_flat[:, 0:E * HID].rearrange("p (e h) -> p e h", h=HID)
        gate_b_col = sb("gate_b_col", [P, 1])

        psum = ctx.enter_context(nc.psum_tensor("psum", [P, 8, 512], F32))

        weights_in = sem("weights_in")
        filled = sem("filled")
        setup_pe = sem("setup_pe")
        setup_dve = sem("setup_dve")
        weights_ready = sem("weights_ready")
        pool_gate = sem("pool_gate")
        act_gate = sem("act_gate")
        dve_gate = sem("dve_gate")
        sp_gate = sem("sp_gate")
        x_loaded = [sem(f"x_loaded{i}") for i in range(GU)]
        bn_done = sem("bn_done")
        dev_ready = sem("dev_ready")
        norm_ready = sem("norm_ready")
        xt_psum = sem("xt_psum")
        xt_ready = sem("xt_ready")
        std_psum = sem("std_psum")
        std_ready = sem("std_ready")
        proj_ready = sem("proj_ready")
        proj_copied = sem("proj_copied")
        prod_ready = sem("prod_ready")
        scaled = sem("scaled")
        ab_ready = sem("ab_ready")
        a_stored = [sem(f"a_stored{i}") for i in range(2)]
        norm_stored = [sem(f"norm_stored{i}") for i in range(2)]
        xq_loaded = [sem(f"xq_loaded{i}") for i in range(QU)]
        y_stored = [sem(f"y_stored{i}") for i in range(QU)]
        a_loaded = [sem(f"a_loaded{i}") for i in range(2)]
        norm_loaded = sem("norm_loaded")
        norm_copied = sem("norm_copied")
        at_psum = sem("at_psum")
        at_ready = sem("at_ready")
        z_psum = sem("z_psum")
        z_ready = sem("z_ready")
        z_squared = sem("z_squared")
        z_summed = sem("z_summed")
        zn_ready = sem("zn_ready")
        znt_psum = sem("znt_psum")
        znt_ready = sem("znt_ready")
        xq_norm = sem("xq_norm")
        xq_psum = sem("xq_psum")
        xqt_ready = sem("xqt_ready")
        g_psum = sem("g_psum")
        gate_ready = sem("gate_ready")
        h_psum = sem("h_psum")
        gated = sem("gated")
        y_ready = sem("y_ready")
        y_psum = sem("y_psum")
        yt_ready = sem("yt_ready")
        ybn_done = sem("ybn_done")
        l_psum = sem("l_psum")
        logit_ready = sem("logit_ready")
        lt_psum = sem("lt_psum")
        cand_done = sem("cand_done")
        exp_done = sem("exp_done")
        cand_stored = sem("cand_stored")
        ends = sem("ends")
        cand_back = sem("cand_back")
        last_in = sem("last_in")
        mine_ready = sem("mine_ready")
        pair_in = sem("pair_in")
        send_ready = sem("send_ready")
        got_in = sem("got_in")
        h1_done = sem("h1_done")
        tail_pool = sem("tail_pool")
        cell_ready = sem("cell_ready")
        cleared = sem("cleared")
        places_in = sem("places_in")
        tok_ready = sem("tok_ready")
        rows_in = sem("rows_in")
        final_ready = sem("final_ready")
        rows_out = sem("rows_out")
        neg_ready = sem("neg_ready")
        ex_ready = sem("ex_ready")
        hpre_ready = sem("hpre_ready")
        ht_ready = sem("ht_ready")
        diag_ready = sem("diag_ready")
        tok_row_psum = sem("tok_row_psum")
        same_ready = sem("same_ready")
        rows_ready = sem("rows_ready")
        pooled_psum = sem("pooled_psum")
        pooled_ready = sem("pooled_ready")
        hid_ready = sem("hid_ready")
        ht_psum = sem("ht_psum")
        count_psum = sem("count_psum")
        o_psum = sem("o_psum")
        ot_ready = sem("ot_ready")
        yadd_ready = sem("yadd_ready")
        w1_in = sem("w1_in")
        w2_in = [sem(f"w2_in{c}") for c in range(EC)]

        block = ctx.enter_context(nc.Block())

        def runs(edge, u, lag):
            return edge is None or (u >= lag if edge == "first" else u < lag)

        def rounds(eng, n, body):
            body(0, "first")
            with eng.Fori(1, n) as r:
                body(r, None)
            body(n, "last")

        def slabs(eng, fill, body, last_body=None, first_body=None):
            def slab(h, start, body):
                at = h * RS
                if start == 0 and first_body:
                    first_body(at, h, 0, None)
                    start = 1
                if start == 1:
                    body(at + 1, h, 1, None)
                    start = 2
                with eng.Fori(start // 2, RS // 2) as two:
                    body(at + two * 2, h, two * 2, None)
                    body(at + two * 2 + 1, h, two * 2 + 1, None)

            fill(0)
            body(0, 0, 0, "first")
            slab(0, 1, body)
            if NSLAB > 2:
                with eng.Fori(1, NSLAB - 1) as h:
                    fill(h)
                    slab(h, 0, body)
            fill(NSLAB - 1)
            slab(NSLAB - 1, 0, last_body or body)
            body(NROUND, NSLAB, 0, "last")

        def group_at(n):
            return (n >> LGB) & (NBLK - 1), n & (GB - 1)

        def quad_at(n):
            return (n >> LQB) & (NBLK - 1), n & (QB - 1)

        def load_a(eng, h, pair):
            for c in range(2):
                eng.dma_start(a_in[:, pair % 2, c], a_slab[(h >> LSB) & (NBLK - 1), :, :, 2 * pair + c, :]
                              ).then_inc(a_loaded[pair % 2], 16)

        WEIGHT_DMAS = 5 + 4 + 1 + 2 + 1 + 1 + 3 * GT

        @block.sync
        def _(sp):
            for g in range(GU):
                sp.dma_start(x_in[:, g], x_groups[0, g]).then_inc(x_loaded[g], 16)
            for i, w in enumerate((Wa1, Wb1, Wa2, Wb2)):
                sp.dma_start(w_raw[:, i * C:(i + 1) * C], w).then_inc(weights_in, 16)
            sp.dma_start(w_raw[:, 4 * C:4 * C + CZ], Wg).then_inc(weights_in, 16)
            for i, v in enumerate((ba1, bb1, ba2, bb2)):
                sp.dma_start(bias_rep[0:GT, i * C:(i + 1) * C],
                             v.unsqueeze(0).to_broadcast([GT, C])).then_inc(weights_in, 16)
            sp.dma_start(bg_row[0:1, :], bg.unsqueeze(0)).then_inc(weights_in, 16)
            for half in range(2):
                sp.dma_start(gate_b_col[half * E:(half + 1) * E, :], gate_b.unsqueeze(1)).then_inc(weights_in, 16)
            sp.dma_start(gw_raw[0:E, :], gate_w).then_inc(weights_in, 16)
            sp.dma_start(bz_row[0:1, :], bz.unsqueeze(0)).then_inc(weights_in, 16)

            with sp.Fori(1, NG // GU) as r:
                for u in range(GU):
                    n = r * GU + u
                    sp.wait_ge(xt_psum, n - GU + 1)
                    sp.wait_ge(bn_done, n - GU + 1)
                    sp.sem_inc(sp_gate, 1)
                    sp.dma_start(x_in[:, u], x_groups[group_at(n)]).then_inc(x_loaded[u], 16)
                    if u % BATCH == BATCH - 1:
                        par = u // BATCH
                        sp.wait_ge(norm_ready, r * 2 - 1 + par)
                        sp.sem_inc(sp_gate, 1)
                        sp.dma_start(norm_dram[r * 2 - 2 + par], norm1[:, par, 0:2]).then_inc(norm_stored[par], 16)
            for par in range(2):
                sp.wait_ge(norm_ready, NBATCH - 1 + par)
                sp.dma_start(norm_dram[NBATCH - 2 + par], norm1[:, par, 0:2]).then_inc(norm_stored[par], 16)

            sp.wait_ge(ab_ready, NG)
            for par in range(2):
                sp.wait_ge(norm_stored[par], NBATCH // 2 * 16)
                sp.wait_ge(a_stored[par], NBATCH // 2 * 16)
            load_a(sp, 0, 0)
            load_a(sp, 0, 1)

            def fill(h):
                since(sp, norm_copied, h * RS)
                sp.sem_inc(sp_gate, 1)
                sp.dma_start(norm_s, norm_slab[h]).then_inc(norm_loaded, 16)

            def body(r, h, rr, edge):
                for u in range(QU):
                    m = r * QU + u
                    if runs(edge, u, 7):
                        q, v = m - 7, (u - 7) % QU
                        sp.wait_ge(y_ready, q + 1)
                        sp.sem_inc(sp_gate, 1)
                        sp.dma_start(out_quads[quad_at(q)], xq[:, v]).then_inc(y_stored[v], 16)
                    if edge == "last":
                        continue
                    if edge is None:
                        sp.wait_ge(y_psum, m - QU + 1)
                        sp.wait_ge(ybn_done, m - QU + 1)
                        sp.sem_inc(sp_gate, 1)
                        sp.wait_ge(y_stored[u], r * 16)
                        sp.sem_inc(sp_gate, 1)
                    sp.dma_start(xq[:, u], x_quads[quad_at(m)]).then_inc(xq_loaded[u], 16)

            slabs(sp, fill, body)
            for u in range(QU):
                sp.wait_ge(y_stored[u], NROUND * 16)

            sp.wait_ge(cand_stored, NROUND * 32)
            sp.wait_ge(ends, 4)
            sp.dma_start(cand_all, cand_dram).then_inc(cand_back, 16)
            sp.dma_start(w1_last[0:E], weight1[:, CZ, :]).then_inc(last_in, 16)
            for half in range(2):
                sp.dma_start(w2_last[half * E:(half + 1) * E], weight2[:, HID, :]).then_inc(last_in, 16)
            sp.wait_ge(mine_ready, 1)
            sp.dma_start(pair[0:E, 1], mine[E:2 * E]).then_inc(pair_in, 16)
            sp.wait_ge(send_ready, 1)
            sp.dma_start(got[E:2 * E], send[0:E, 1]).then_inc(got_in, 16)
            for c in range(EC):
                sp.wait_ge(h1_done, c + 1)
                sp.dma_start(w_sb[:, c * EG:(c + 1) * EG].rearrange("p e (g o) -> p e g o", g=4),
                             weight2[c * EG:(c + 1) * EG, 0:HID, :].rearrange("e (p g) o -> p e g o", g=4)
                             ).then_inc(w2_in[c], 16)

        @block.gpsimd
        def _(pool):
            G = nc.gpsimd
            G.memset(ident[:, :], 0.0).then_inc(filled, 1)
            G.memset(blockmean, 1.0 / C).then_inc(filled, 1)
            G.memset(ones_row, 1.0 / CZ).then_inc(filled, 1)
            G.memset(neg_mean, -1.0 / CZ).then_inc(filled, 1)
            pool.wait_ge(filled, 4)
            G.affine_select(out=ident[:, :], in_=ident[:, :], compare_op=ALU.not_equal, fill=1.0,
                            base=0, pattern=[[-1, P]], channel_multiplier=1).then_inc(filled, 1)
            bm = blockmean.rearrange("p (j c) -> p j c", c=C)
            G.affine_select(out=bm, in_=bm, compare_op=ALU.is_ge, fill=0.0, base=0,
                            pattern=[[-C, GT], [0, C]], channel_multiplier=1).then_inc(filled, 1)
            pool.wait_ge(filled, 6)
            G.affine_select(out=bm, in_=bm, compare_op=ALU.is_ge, fill=0.0, base=C - 1,
                            pattern=[[C, GT], [0, C]], channel_multiplier=-1).then_inc(filled, 1)

            def first_round(r):
                for u in range(GU):
                    m = r * GU + u
                    par, i = u // BATCH, (u % BATCH) * GT
                    pool.wait_ge(proj_copied, m + 1)
                    since(pool, ab_ready, m - 3)
                    pool.sem_inc(pool_gate, 1)
                    G.tensor_tensor(prod1[:, u % 4], proj1[:, u % 4, :, 0:2 * C], proj1[:, u % 4, :, 2 * C:4 * C],
                                    ALU.mult).then_inc(prod_ready, 1)
                    pool.wait_ge(norm_ready, r * 2 + par + 1)
                    pool.wait_ge(prod_ready, m + 1)
                    pool.sem_inc(pool_gate, 1)
                    G.tensor_tensor(prod1[:, u % 4], prod1[:, u % 4],
                                    norm1[:, par, 3, i:i + GT].unsqueeze(2).to_broadcast([P, GT, 2 * C]),
                                    ALU.mult).then_inc(scaled, 1)

            first_round(0)
            with pool.Fori(1, NG // GU) as r:
                first_round(r)

            pool.wait_ge(ab_ready, NG)

            def normalise_x(r, h, rr, u, m):
                if u == 0:
                    pool.wait_ge(norm_loaded, (h + 1) * 16)
                    since(pool, xq_norm, m)
                    pool.sem_inc(pool_gate, 1)
                    G.tensor_copy(norm_r, norm_s[:, rr]).then_inc(norm_copied, 1)
                    pool.wait_ge(norm_copied, r + 1)
                    pool.sem_inc(pool_gate, 1)
                pool.wait_ge(xq_loaded[u], (r + 1) * 16)
                since(pool, xq_psum, m - 1)
                pool.sem_inc(pool_gate, 1)
                for t in range(QT):
                    i = u * QT + t
                    last = G.tensor_scalar(xh2[:, u % 2, t], xq[:, u, t], norm_r[:, 0, i:i + 1],
                                           norm_r[:, 1, i:i + 1], ALU.mult, ALU.add)
                last.then_inc(xq_norm, 1)

            def body(r, h, rr, edge):
                for u in range(QU):
                    m = r * QU + u
                    if edge != "last":
                        normalise_x(r, h, rr, u, m)
                    if runs(edge, u, 4):
                        q, v = m - 4, (u - 4) % QU
                        pool.wait_ge(gated, q + 1)
                        G.tensor_tensor(xq[:, v], xq[:, v], gate[:, v % 4], ALU.add).then_inc(y_ready, 1)

            slabs(pool, lambda h: None, body)

            pool.drain()
            pool.sem_inc(ends, 1)
            pool.wait_ge(ends, 4)
            G.iota(iota16.bitcast(I32), pattern=[[1, 2 * K]], base=0, channel_multiplier=0).then_inc(tail_pool, 1)
            G.iota(base_col.bitcast(I32), pattern=[[0, 1]], base=0, channel_multiplier=NCH * K).then_inc(tail_pool, 1)
            G.memset(ones_m, 1.0).then_inc(tail_pool, 1)
            G.memset(before, 1.0).then_inc(tail_pool, 1)
            pool.wait_ge(tail_pool, 4)
            G.affine_select(out=before, in_=before, compare_op=ALU.is_gt, fill=0.0,
                            base=0, pattern=[[1, P]], channel_multiplier=-1).then_inc(tail_pool, 1)
            pool.wait_ge(cell_ready, 1)
            for k in range(K):
                pool.indirect_dma_start(out=place_got[:, k:k + 1], out_offset=None, in_=place_cells,
                                        in_offset=bass.IndirectOffsetOnAxis(ap=cell[:, k:k + 1], axis=0)
                                        ).then_inc(places_in, 16)
            pool.wait_ge(tok_ready, 1)
            for k in range(K // 2):
                pool.indirect_dma_start(out=rows[:, k], out_offset=None, in_=out_rows,
                                        in_offset=bass.IndirectOffsetOnAxis(ap=tok_u[:, k:k + 1], axis=0)
                                        ).then_inc(rows_in, 16)
            G.memset(pooled1, 0.0).then_inc(cleared, 1)
            G.memset(hidden4, 0.0).then_inc(cleared, 1)
            pool.wait_ge(final_ready, 1)
            for k in range(K // 2):
                pool.indirect_dma_start(out=out_rows,
                                        out_offset=bass.IndirectOffsetOnAxis(ap=tok_w[:, k:k + 1], axis=0),
                                        in_=rows[:, k], in_offset=None, bounds_check=N * N - 1, oob_is_err=False
                                        ).then_inc(rows_out, 16)
            pool.wait_ge(rows_out, 16 * K // 2)

        @block.scalar
        def _(act):
            A = nc.scalar
            for j in range(GT):
                act.dma_start(wz_raw[j * C:(j + 1) * C, :], Wz).then_inc(weights_in, 16)
                act.dma_start(ln2_col[j * C:(j + 1) * C, 0:1], ln2_g.unsqueeze(1)).then_inc(weights_in, 16)
                act.dma_start(ln2_col[j * C:(j + 1) * C, 1:2], ln2_b.unsqueeze(1)).then_inc(weights_in, 16)

            def first_round(r, edge):
                for u in range(GU):
                    n = r * GU + u
                    if edge != "last":
                        if u % BATCH == 0:
                            batch = r * 2 + u // BATCH
                            act.wait_ge(std_psum, batch + 1)
                            A.activation(stdT[0:GT, u // BATCH], psum[0:GT, 7, :].rearrange("p (b q) -> p b q", b=BATCH),
                                         ACT.Copy).then_inc(std_ready, 1)
                        act.wait_ge(xt_psum, n + 1)
                        since(act, proj_ready, n - 1)
                        A.activation(xT1[:, u % 2, :], psum[:, 2 * (u % 2):2 * (u % 2) + 2, :],
                                     ACT.Copy).then_inc(xt_ready, 1)
                    if runs(edge, u, 2):
                        m, v = n - 2, (u - 2) % GU
                        act.wait_ge(proj_ready, m + 1)
                        since(act, prod_ready, m - 3)
                        A.activation(proj1[:, v % 4], psum[:, 4 + v % 4, :].rearrange("p (t c) -> p t c", t=GT),
                                     ACT.Copy).then_inc(proj_copied, 1)
                    if runs(edge, u, 4):
                        m, v = n - 4, (u - 4) % GU
                        par = v // BATCH
                        act.wait_ge(scaled, m + 1)
                        if v % BATCH == 0:
                            since(act, a_stored[par], (r if u >= 4 else r - 1) * 16)
                        act.sem_inc(act_gate, 1)
                        col = (v % BATCH) * GT
                        A.activation(a_out[:, par, :, col:col + GT].rearrange("p c s -> p s c"),
                                     prod1[:, v % 4, :, 0:C], ACT.Sigmoid)
                        blk, g = group_at(m)
                        A.activation(b_all[:, blk, :, bass.ds(g * GT, GT)].rearrange("p c s -> p s c"),
                                     prod1[:, v % 4, :, C:2 * C], ACT.Sigmoid).then_inc(ab_ready, 1)
                        if v % BATCH == BATCH - 1:
                            act.wait_ge(ab_ready, m + 1)
                            act.sem_inc(act_gate, 1)
                            act.dma_start(a_dram[((m - (BATCH - 1)) >> 2) & (NBATCH - 1)],
                                          a_out[:, par]).then_inc(a_stored[par], 16)

            rounds(act, NG // GU, first_round)

            def square(h, c):
                act.wait_ge(z_ready, h * C + c + 1)
                since(act, z_summed, h * (C - 1) + c - 2)
                act.sem_inc(act_gate, 1)
                A.activation(z_sq[c % 2], z[:, c, :], ACT.Square).then_inc(z_squared, 1)

            def fill(h):
                for c in range(C):
                    act.wait_ge(at_psum, h * C + c + 1)
                    since(act, z_psum, h * C + c - 1)
                    act.sem_inc(act_gate, 1)
                    A.activation(aT[:, c % 2], psum[:, 7 * (c % 2), 0:NBLK * P].rearrange("p (k i) -> p k i", k=NBLK),
                                 ACT.Copy).then_inc(at_ready, 1)
                    if c % 2 == 1:
                        ahead = c // 2 + 2
                        if ahead < C // 2:
                            load_a(act, h, ahead)
                        elif not (isinstance(h, int) and h == NSLAB - 1):
                            load_a(act, h + 1, ahead - C // 2)
                    if c >= 3:
                        square(h, c - 2)
                square(h, C - 2)
                square(h, C - 1)
                if isinstance(h, int) and h == NSLAB - 1:
                    act.wait_ge(z_psum, NSLAB * C)

            def body(r, h, rr, edge, brings_w1=False):
                for u in range(QU):
                    n = r * QU + u
                    for i in range(E // QS if brings_w1 else 0):
                        e = rr * (E // RS) + u * (E // QS) + i
                        act.dma_start(w_sb[:, e], weight1[e, 0:CZ, :]).then_inc(w1_in, 16)
                    if edge != "last":
                        act.wait_ge(xq_psum, n + 1)
                        since(act, g_psum, n - 1)
                        A.activation(xT2[:, u % 2], psum[:, 0, :], ACT.Copy).then_inc(xqt_ready, 1)
                    if runs(edge, u, 1):
                        q, v = n - 1, (u - 1) % QU
                        act.wait_ge(g_psum, q + 1)
                        since(act, y_ready, q - 3)
                        A.activation(gate[:, v % 4], psum[:, 2, :].rearrange("p (t c) -> p t c", t=QT),
                                     ACT.Tanh, scale=0.5).then_inc(gate_ready, 1)
                    if u == 1 and edge != "last":
                        act.wait_ge(znt_psum, r + 1)
                        A.activation(znT, psum[:, 1, 0:RT * C].rearrange("p (g i) -> p g i", i=P),
                                     ACT.Copy, bias=1.0).then_inc(znt_ready, 1)
                    if runs(edge, u, 5):
                        q = n - 5
                        act.wait_ge(y_psum, q + 1)
                        since(act, l_psum, q)
                        A.activation(yT, psum[:, 1, :], ACT.Copy).then_inc(yt_ready, 1)
                    if u % 2 == 1 and edge != "first":
                        s, k = u // 2, (r - 1) * (QU // 2) + u // 2
                        since(act, cand_stored, (r - 1) * 32)
                        act.wait_ge(cand_done, k + 1)
                        act.sem_inc(act_gate, 1)
                        A.activation(psum[:, 7, :], psum[:, 7, :], ACT.Exp, bias=negmax[:, s],
                                     accum_out=cand[:, s, K:K + 1]).then_inc(exp_done, 1)
                        if u == QU - 1:
                            act.wait_ge(exp_done, r * (QU // 2))
                            act.sem_inc(act_gate, 1)
                            at = bass.ds((r - 1) * (QU // 2), QU // 2)
                            act.dma_start(cand_dram[:, at, :], cand).then_inc(cand_stored, 16)
                            act.dma_start(place_dram[:, at, :], place).then_inc(cand_stored, 16)

            def last_body(r, h, rr, edge):
                body(r, h, rr, edge, brings_w1=True)

            slabs(act, fill, body, last_body)
            act.wait_ge(cand_stored, NROUND * 32)

            act.sem_inc(ends, 1)
            act.wait_ge(neg_ready, 1)
            A.activation(ex_all, cand_v.rearrange("p (n k) -> p n k", k=K)[:, :, 0], ACT.Exp, bias=mine[:, 2 * K:2 * K + 1]).then_inc(ex_ready, 1)
            act.wait_ge(neg_ready, 2)
            A.activation(small[0:E, 2:4], small[0:E, 0:2], ACT.Exp).then_inc(ex_ready, 1)
            A.activation(top_v[0:E], top_v[0:E], ACT.Exp, bias=small[0:E, 4:5]).then_inc(ex_ready, 1)
            act.wait_ge(hpre_ready, 1)
            A.activation(hid[0:E], hpre[0:E], ACT.Gelu).then_inc(hid_ready, 1)

        @block.vector
        def _(dve):
            V = nc.vector
            dve.wait_ge(weights_in, 16 * WEIGHT_DMAS)
            dve.wait_ge(filled, 7)
            V.tensor_scalar(wz_fold, wz_raw, ln2_col[:, 0:1], 0.5, ALU.mult, ALU.mult)
            V.tensor_scalar(wz_bias, wz_raw, ln2_col[:, 1:2], 0.5, ALU.mult, ALU.mult)
            V.tensor_scalar(bz_row[0:1, :], bz_row[0:1, :], CZ / (2.0 * C), None, ALU.mult)
            for t in range(GT):
                V.tensor_scalar(bias1[0:GT, t, :], bias_rep[0:GT, :], ident[0:GT, t:t + 1], None, ALU.mult)
            V.drain()
            V.tensor_tensor(wz_bias, wz_bias, wz_fold, ALU.subtract)
            dve.wait_ge(setup_pe, 1)
            V.tensor_copy(w_raw[:, 4 * C + CZ:NW], psum[:, 0, 0:E])
            V.drain().then_inc(setup_dve, 1)
            dve.wait_ge(setup_pe, 3)
            V.tensor_tensor(w_proj[:, :], w_raw[:, 0:4 * C], psum[:, 1, 0:4 * C], ALU.add)
            V.tensor_tensor(w_gate[:, :], w_raw[:, 4 * C:4 * C + CZ], psum[:, 1, 4 * C:4 * C + CZ], ALU.add)
            V.tensor_tensor(w_exp[:, :], w_raw[:, 4 * C + CZ:NW], psum[:, 1, 4 * C + CZ:NW], ALU.add)
            V.tensor_tensor(wz_fold, wz_fold, psum[:, 2, 0:CZ], ALU.add)
            V.drain()
            V.tensor_scalar(wz_fold, wz_fold, float(C), None, ALU.mult)
            V.drain()
            for j in range(GT):
                V.tensor_scalar(w_z[:, j, :], wz_fold, blockmean[:, j * C:j * C + 1], None, ALU.mult)
            V.drain().then_inc(weights_ready, 1)

            def rsqrt(v, y, t):
                V.tensor_scalar(t.bitcast(I32), v.bitcast(I32), 1, None, ALU.arith_shift_right)
                V.drain()
                V.tensor_scalar(y.bitcast(I32), t.bitcast(I32), -1.0, float(RSQRT_MAGIC), ALU.mult, ALU.add)
                for _ in range(3):
                    V.drain()
                    V.tensor_tensor(t, y, y, ALU.mult)
                    V.drain()
                    V.scalar_tensor_tensor(t, t, -0.5, v, ALU.mult, ALU.mult)
                    V.drain()
                    V.scalar_tensor_tensor(y, t, 1.5, y, ALU.add, ALU.mult)
                V.drain()

            def scales(st, tmp, root, eps, twice_mean=None):
                even, odd = st[:, :, 1], st[:, :, 4]
                V.drain()
                V.tensor_tensor(tmp[:, 0], even, odd, ALU.subtract)
                V.scalar_tensor_tensor(tmp[:, 2], st[:, :, 2], CZ * eps, st[:, :, 5], ALU.add, ALU.add)
                if twice_mean is not None:
                    V.tensor_tensor(twice_mean, even, odd, ALU.add)
                V.drain()
                V.scalar_tensor_tensor(tmp[:, 3], tmp[:, 0], CZ / 4.0, tmp[:, 0], ALU.mult, ALU.mult)
                V.drain()
                V.tensor_tensor(tmp[:, 1], tmp[:, 2], tmp[:, 3], ALU.add)
                V.drain()
                rsqrt(tmp[:, 1], root, tmp[:, 2])

            root1, mean1 = tmp1[:, 4], tmp1[:, 5]

            def first_round(r):
                for u in range(GU):
                    n = r * GU + u
                    par = u // BATCH
                    dve.wait_ge(x_loaded[u], (r + 1) * 16)
                    for t in range(GT):
                        last = V.bn_stats(st1[:, (u % BATCH) * GT + t], x_in[:, u, t])
                    last.then_inc(bn_done, 1)
                    if u % BATCH == BATCH - 1:
                        scale, shift, std, scale2 = (norm1[:, par, i] for i in range(4))
                        scales(st1, tmp1, root1, EPS_C, mean1)
                        since(dve, std_psum, r * 2 + par - 1)
                        dve.sem_inc(dve_gate, 1)
                        V.scalar_tensor_tensor(std, tmp1[:, 1], 1 / ROOT_CZ, root1, ALU.mult, ALU.mult
                                               ).then_inc(dev_ready, 1)
                        since(dve, norm_stored[par], r * 16)
                        since(dve, scaled, n - GU + 1)
                        dve.sem_inc(dve_gate, 1)
                        V.scalar_tensor_tensor(scale2, root1, float(CZ), root1, ALU.mult, ALU.mult)
                        V.tensor_scalar(scale, root1, ROOT_CZ, None, ALU.mult)
                        V.scalar_tensor_tensor(tmp1[:, 3], mean1, -0.5 * ROOT_CZ, root1, ALU.mult, ALU.mult)
                        V.drain()
                        V.tensor_scalar(shift, tmp1[:, 3], 1.0, None, ALU.add).then_inc(norm_ready, 1)

            first_round(0)
            with dve.Fori(1, NG // GU) as r:
                first_round(r)

            dve.wait_ge(ab_ready, NG)

            def fill(h):
                for c in range(C + 1):
                    if c < C:
                        dve.wait_ge(z_psum, h * C + c + 1)
                    if c == 0:
                        V.tensor_copy(z[:, 0, :], psum[:, 1, 0:SLAB]).then_inc(z_ready, 1)
                    elif c < C:
                        V.tensor_tensor(z[:, c, :], psum[:, 1 + c % 2, 0:SLAB], z[:, 0, :], ALU.subtract
                                        ).then_inc(z_ready, 1)
                    V.drain()
                    if c == 1:
                        V.tensor_copy(z_sum, z[:, 1, :])
                    elif 1 < c < C:
                        V.tensor_tensor(z_sum, z_sum, z[:, c, :], ALU.add)
                    if c >= 2:
                        dve.wait_ge(z_squared, h * (C - 1) + c - 1)
                        if c == 2:
                            V.tensor_copy(z_var, z_sq[1]).then_inc(z_summed, 1)
                        else:
                            V.tensor_tensor(z_var, z_var, z_sq[(c - 1) % 2], ALU.add).then_inc(z_summed, 1)
                V.memset(z[:, 0, :], 0.0)

            def finish_z():
                V.scalar_tensor_tensor(z_tmp, z_sum, -1.0 / C, z_sum, ALU.mult, ALU.mult)
                V.drain()
                V.tensor_tensor(z_var, z_var, z_tmp, ALU.add)
                V.drain()
                V.tensor_scalar(z_var, z_var, 1.0 / C, EPS_T, ALU.mult, ALU.add)
                V.drain()
                rsqrt(z_var, z_scale, z_tmp)

            def body(r, h, rr, edge, opens_slab=False):
                for u in range(QU):
                    n = r * QU + u
                    if u % 2 == 0 and edge != "first":
                        k = (r - 1) * (QU // 2) + u // 2
                        dve.wait_ge(l_psum, n - 6)
                        since(dve, lt_psum, k)
                        root = yroot[:, u // 4, (u // 2 % 2) * 2 * QT:(u // 2 % 2 + 1) * 2 * QT]
                        V.scalar_tensor_tensor(logit, psum[:, 6 - 3 * (u // 2 % 2), :].rearrange("p (t e) -> p t e", e=E), ROOT_CZ,
                                               root.unsqueeze(2).to_broadcast([P, 2 * QT, E]),
                                               ALU.mult, ALU.mult).then_inc(logit_ready, 1)
                    if runs(edge, u, 3):
                        q, v = n - 3, (u - 3) % QU
                        dve.wait_ge(gate_ready, q + 1)
                        dve.wait_ge(h_psum, q + 1)
                        V.scalar_tensor_tensor(gate[:, v % 4], gate[:, v % 4], 1.0,
                                               psum[:, 4 + v % 2, :].rearrange("p (t c) -> p t c", t=QT),
                                               ALU.add, ALU.mult).then_inc(gated, 1)
                    if runs(edge, u, 4):
                        q, v = n - 4, (u - 4) % QU
                        dve.wait_ge(y_ready, q + 1)
                        for t in range(QT):
                            last = V.bn_stats(st2[:, v % QB2 * QT + t], xq[:, v, t])
                        last.then_inc(ybn_done, 1)
                    if u % 2 == 1 and edge != "first":
                        s, k = u // 2, (r - 1) * (QU // 2) + u // 2
                        dve.wait_ge(lt_psum, k + 1)
                        since(dve, cand_stored, (r - 1) * 32)
                        dve.sem_inc(dve_gate, 1)
                        V.max(out=cand[:, s, 0:K], in_=psum[:, 7, :])
                        V.drain()
                        V.tensor_scalar(negmax[:, s], cand[:, s, 0:1], -1.0, None, ALU.mult)
                        V.max_index(out=place[:, s], in_max=cand[:, s, 0:K], in_values=psum[:, 7, :])
                        V.drain().then_inc(cand_done, 1)
                    if u == 0 and edge != "last":
                        if opens_slab or edge == "first":
                            finish_z()
                        since(dve, znt_psum, r)
                        at = bass.ds(rr * RT, RT)
                        V.scalar_tensor_tensor(zn, z_sum[:, at].unsqueeze(2).to_broadcast([P, RT, C]), -1.0 / C,
                                               z[:, :, at].rearrange("p c s -> p s c"), ALU.mult, ALU.add)
                        V.drain()
                        V.tensor_tensor(zn, zn, z_scale[:, at].unsqueeze(2).to_broadcast([P, RT, C]),
                                        ALU.mult).then_inc(zn_ready, 1)
                    if u % QB2 == 3 and runs(edge, u, 4):
                        scales(st2, tmp2, yroot[:, (u - 4) % QU // QB2], EPS_T)

            def first_body(r, h, rr, edge):
                body(r, h, rr, edge, opens_slab=True)

            slabs(dve, fill, body, first_body=first_body)

            V.drain().then_inc(ends, 1)
            dve.wait_ge(tail_pool, 5)
            dve.wait_ge(cand_back, 16)
            V.tensor_copy(iota16, iota16.bitcast(I32))
            V.tensor_copy(base_col, base_col.bitcast(I32))
            V.memset(parity, 0)
            V.tensor_tensor(pick, ident[:, 0:E], ident[:, E:2 * E], ALU.add)
            V.tensor_scalar(cand_v.rearrange("p (n k) -> p n k", k=K), cand_all[:, :, 0:K], gate_b_col[:, :], None, ALU.add)
            V.drain()
            V.max(out=best, in_=cand_v)
            V.drain()
            V.memset(parity[E:2 * E], 1)
            V.max_index(out=best_at, in_max=best, in_values=cand_v)
            V.tensor_copy(mine[:, 0:K], best)
            V.tensor_scalar(mine[:, 2 * K:2 * K + 1], best[:, 0:1], -1.0, None, ALU.mult).then_inc(neg_ready, 1)
            V.drain()
            V.tensor_copy(cell_f, best_at)
            V.drain()
            V.tensor_scalar(cell_f, cell_f, base_col, None, ALU.add)
            V.drain()
            V.tensor_copy(cell, cell_f)
            V.drain().then_inc(cell_ready, 1)
            dve.wait_ge(ex_ready, 1)
            V.tensor_tensor(ex_all, ex_all, cand_all[:, :, K], ALU.mult)
            V.drain()
            V.tensor_reduce(out=mine[:, 2 * K + 1:2 * K + 2], in_=ex_all, op=ALU.add, axis=AX.X)
            V.tensor_scalar(tok_a, best_at, LN, LN + 7, ALU.logical_shift_right, ALU.logical_shift_left)
            V.tensor_scalar(tok_b, best_at, N - GT, None, ALU.bitwise_and)
            V.drain()
            V.tensor_tensor(tok_a, tok_a, tok_b, ALU.bitwise_or)
            dve.wait_ge(places_in, 16 * K)
            V.drain()
            V.tensor_scalar(tok_b, place_got, P - 1, LN, ALU.bitwise_and, ALU.logical_shift_left)
            V.drain()
            V.tensor_tensor(tok_a, tok_a, tok_b, ALU.bitwise_or)
            V.drain()
            V.tensor_scalar(tok_b, place_got, 7, 1, ALU.logical_shift_right, ALU.logical_shift_left)
            V.drain()
            V.tensor_tensor(tok_a, tok_a, tok_b, ALU.bitwise_or)
            V.drain()
            V.tensor_tensor(tok_a, tok_a, parity.to_broadcast([P, K]), ALU.bitwise_or)
            V.drain()
            V.tensor_copy(mine[:, K:2 * K], tok_a)
            V.drain().then_inc(mine_ready, 1)
            dve.wait_ge(pair_in, 16)
            V.tensor_copy(pair[0:E, 0], mine[0:E])
            V.drain()
            V.tensor_copy(pair_v[0:E].rearrange("p (a k) -> p a k", a=2), pair[0:E, :, 0:K])
            V.drain()
            V.max(out=top_v[0:E], in_=pair_v[0:E])
            V.drain()
            V.max_index(out=top_at[0:E], in_max=top_v[0:E], in_values=pair_v[0:E])
            V.tensor_scalar(small[0:E, 4:5], top_v[0:E, 0:1], -1.0, None, ALU.mult)
            V.drain()
            V.tensor_copy(top_at_f[0:E], top_at[0:E])
            V.scalar_tensor_tensor(small[0:E, 0:2], pair[0:E, :, 2 * K], -1.0,
                                   small[0:E, 4:5].to_broadcast([E, 2]), ALU.mult, ALU.add)
            V.drain().then_inc(neg_ready, 1)
            V.tensor_tensor(hot[0:E], iota16[0:E].unsqueeze(1).to_broadcast([E, K, 2 * K]),
                            top_at_f[0:E].unsqueeze(2).to_broadcast([E, K, 2 * K]), ALU.is_equal)
            V.drain()
            for a in range(2):
                V.tensor_tensor(hot[0:E, :, a * K:(a + 1) * K], hot[0:E, :, a * K:(a + 1) * K],
                                pair[0:E, a, K:2 * K].unsqueeze(1).to_broadcast([E, K, K]), ALU.mult)
            dve.wait_ge(ex_ready, 3)
            V.drain()
            V.tensor_reduce(out=send[0:E, :, 0].rearrange("p a k -> p k a"),
                            in_=hot[0:E].rearrange("p (k a) m -> p k a m", a=2), op=ALU.add, axis=AX.X)
            V.tensor_tensor(small[0:E, 2:4], small[0:E, 2:4], pair[0:E, :, 2 * K + 1], ALU.mult)
            V.drain()
            V.tensor_tensor(small[0:E, 5:6], small[0:E, 2:3], small[0:E, 3:4], ALU.add)
            V.drain()
            V.reciprocal(small[0:E, 6:7], small[0:E, 5:6])
            V.drain()
            V.tensor_scalar(send[0:E, :, 1].rearrange("p a k -> p k a"),
                            top_v[0:E].rearrange("p (k a) -> p k a", a=2), small[0:E, 6:7], None, ALU.mult)
            V.drain()
            V.tensor_copy(got[0:E], send[0:E, 0])
            V.drain().then_inc(send_ready, 1)
            dve.wait_ge(got_in, 16)
            V.tensor_copy(tok_u, got[:, 0])
            V.drain().then_inc(tok_ready, 1)
            for k in range(K // 2):
                V.tensor_scalar(diag[:, k], ident[:, :], got[:, 0, k:k + 1], None, ALU.mult)
            V.drain().then_inc(diag_ready, 1)
            dve.wait_ge(tok_row_psum, 1)
            V.tensor_copy(tok_row, psum[:, 0, :].rearrange("p (k q) -> p k q", q=P))
            V.drain()
            for s in range(K // 2):
                for t in range(K // 2):
                    V.tensor_scalar(same[:, s, t], tok_row[:, t], got[:, 0, s:s + 1], None, ALU.is_equal)
            V.drain()
            for t in range(K // 2):
                V.tensor_tensor(same_before[:, t], same[:, t, t], before, ALU.mult)
            V.drain().then_inc(same_ready, 1)
            dve.wait_ge(rows_in, 16 * K // 2)
            for k in range(K // 2):
                V.bn_stats(st3[:, k], rows[:, k])
            scales(st3, tmp3, tmp3[:, 4], EPS_T, tmp3[:, 5])
            V.tensor_scalar(norm3[:, 0], tmp3[:, 4], ROOT_CZ, None, ALU.mult)
            V.scalar_tensor_tensor(norm3[:, 1], tmp3[:, 5], -0.5 * ROOT_CZ, tmp3[:, 4], ALU.mult, ALU.mult)
            V.drain()
            for k in range(K // 2):
                V.tensor_scalar(rows_n[:, k], rows[:, k], norm3[:, 0, k:k + 1], norm3[:, 1, k:k + 1], ALU.mult, ALU.add)
            V.drain()
            for k in range(K // 2):
                V.tensor_scalar(rows_n[:, k], rows_n[:, k], got[:, 1, k:k + 1], None, ALU.mult)
            V.drain().then_inc(rows_ready, 1)
            dve.wait_ge(pooled_psum, 1)
            dve.wait_ge(cleared, 2)
            V.tensor_copy(pooled1[:, :, bass.ds(0, 32, 33)], psum[:, 1, 0:E].rearrange("p (j e) -> p j e", j=2))
            V.drain().then_inc(pooled_ready, 1)
            dve.wait_ge(count_psum, 1)
            V.tensor_scalar(tok_wf, psum[:, 5, 0:K // 2], 1.0, float(2 * N * N), ALU.min, ALU.mult)
            V.drain()
            V.tensor_tensor(tok_wf, tok_wf, got[:, 0], ALU.add)
            V.drain()
            V.tensor_copy(tok_w, tok_wf)
            dve.wait_ge(h1_done, EC)
            dve.wait_ge(last_in, 48)
            V.tensor_tensor(hpre[0:E], w1_last[0:E], psum[0:E, 3, :], ALU.add)
            V.tensor_copy(twice[0:E, 0:E], ident[0:E, 0:E])
            V.tensor_copy(twice[0:E, E:2 * E], ident[0:E, 0:E])
            V.drain().then_inc(hpre_ready, 1)
            dve.wait_ge(ht_psum, 1)
            V.tensor_copy(hidden4[:, :, :, bass.ds(0, 32, 33)],
                          psum[:, 2, 0:4 * E].rearrange("p (g j e) -> p g j e", g=4, j=2))
            V.drain().then_inc(ht_ready, 1)
            dve.wait_ge(o_psum, 1)
            V.tensor_copy(o_sb[0:E], psum[0:E, 4, 0:CZ])
            V.drain().then_inc(ot_ready, 1)
            dve.wait_ge(o_psum, 2)
            V.tensor_tensor(o_pair, w2_last, psum[:, 6, 0:CZ], ALU.add)
            V.drain()
            for k in range(K // 2):
                V.tensor_scalar(y_add[:, k], o_pair, got[:, 1, k:k + 1], None, ALU.mult)
            V.drain().then_inc(yadd_ready, 1)
            dve.wait_ge(o_psum, 3)
            V.tensor_tensor(rows, rows, psum[:, 7, :].rearrange("p (k c) -> p k c", c=CZ), ALU.add)
            V.drain().then_inc(final_ready, 1)

        @block.tensor
        def _(pe):
            PE = nc.tensor
            pe.wait_ge(weights_in, 16 * WEIGHT_DMAS)
            pe.wait_ge(filled, 7)
            PE.transpose(psum[:, 0, 0:E], gw_raw[0:E, :], ident[0:E, 0:E]).then_inc(setup_pe, 1)
            pe.wait_ge(setup_dve, 1)
            PE.matmul(psum[:, 1, 0:NW], neg_mean, w_raw, start=True, stop=False)
            PE.matmul(psum[:, 1, 4 * C:4 * C + CZ], ones_row[0:1, :], bg_row[0:1, :],
                      start=False, stop=True).then_inc(setup_pe, 1)
            PE.matmul(psum[:, 2, 0:CZ], blockmean, wz_bias, start=True, stop=False)
            PE.matmul(psum[:, 2, 0:CZ], ones_row[0:1, :], bz_row[0:1, :], start=False, stop=True).then_inc(setup_pe, 1)
            pe.wait_ge(weights_ready, 1)

            def first_round(r, edge):
                for u in range(GU):
                    n = r * GU + u
                    if u % BATCH == 0 and edge != "last":
                        par = u // BATCH
                        pe.wait_ge(dev_ready, r * 2 + par + 1)
                        since(pe, proj_copied, n - 4)
                        for g in range(BATCH):
                            last = PE.transpose(psum[0:GT, 7, g * P:(g + 1) * P],
                                                norm1[:, par, 2, g * GT:(g + 1) * GT], ident[:, :])
                        last.then_inc(std_psum, 1)
                    loads, projects = edge != "last", runs(edge, u, 2)
                    m, v = n - 2, (u - 2) % GU
                    if loads:
                        pe.wait_ge(x_loaded[u], (r + 1) * 16)
                        since(pe, xt_ready, n - 1)
                    if projects:
                        pe.wait_ge(xt_ready, m + 1)
                        since(pe, proj_copied, m - 3)
                        pe.wait_ge(std_ready, r * 2 + ((u - 1) // BATCH + 1 if loads else 0))
                        PE.matmul(psum[:, 4 + v % 4, :], stdT[0:GT, v // BATCH, v % BATCH], bias1[0:GT].rearrange("p t c -> p (t c)"),
                                  start=True, stop=False)
                    for t in range(GT):
                        if loads:
                            xt = PE.transpose(psum[:, 2 * (u % 2) + t // 4, (t % 4) * P:(t % 4 + 1) * P],
                                              x_in[:, u, t], ident[:, :])
                        if projects:
                            pr = PE.matmul(psum[:, 4 + v % 4, t * 4 * C:(t + 1) * 4 * C],
                                           xT1[:, v % 2, t * P:(t + 1) * P], w_proj[:, :],
                                           start=False, stop=(t == GT - 1))
                    if loads:
                        xt.then_inc(xt_psum, 1)
                    if projects:
                        pr.then_inc(proj_ready, 1)

            rounds(pe, NG // GU, first_round)

            pe.wait_ge(ab_ready, NG)

            def fill(h):
                since(pe, xqt_ready, h * QS)
                since(pe, yt_ready, h * QS - 5)
                since(pe, gate_ready, h * QS - 1)
                since(pe, exp_done, (h * RS - 1) * (QU // 2))
                since(pe, cand_done, (h * RS - 1) * (QU // 2))
                for c in range(C + 1):
                    if c < C:
                        pe.wait_ge(a_loaded[c // 2 % 2], (h * (C // 4) + c // 4 + 1) * 32)
                        since(pe, at_ready, h * C + c - 1)
                        for k in range(NBLK):
                            last = PE.transpose(psum[:, 7 * (c % 2), k * P:(k + 1) * P],
                                                a_in[:, c // 2 % 2, c % 2, k * (P // BT):(k + 1) * (P // BT)].rearrange("p t s -> p (t s)"),
                                                ident[:, :])
                        last.then_inc(at_psum, 1)
                    if c >= 1:
                        pe.wait_ge(at_ready, h * C + c)
                        since(pe, z_ready, h * C + c - 2)
                        for k in range(NBLK):
                            last = PE.matmul(psum[:, 1 + (c - 1) % 2, 0:SLAB], aT[:, (c - 1) % 2, k],
                                             b_all[:, k, c - 1, bass.ds((h & (SB - 1)) * SLAB, SLAB)],
                                             start=(k == 0), stop=(k == NBLK - 1))
                        last.then_inc(z_psum, 1)

            def body(r, h, rr, edge):
                for u in range(QU):
                    n = r * QU + u
                    if u % 2 == 1 and edge != "first":
                        k = (r - 1) * (QU // 2) + u // 2
                        pe.wait_ge(logit_ready, k + 1)
                        since(pe, exp_done, k)
                        since(pe, cand_done, k)
                        for g in range(QT):
                            last = PE.transpose(psum[:, 7, g * P:(g + 1) * P],
                                                logit[:, 2 * g:2 * g + 2, :].rearrange("p t e -> p (t e)"), ident[:, :])
                        last.then_inc(lt_psum, 1)
                    if edge != "last":
                        pe.wait_ge(xq_norm, n + 1)
                        since(pe, xqt_ready, n)
                        for t in range(QT):
                            last = PE.transpose(psum[:, 0, t * P:(t + 1) * P], xh2[:, u % 2, t], ident[:, :])
                        last.then_inc(xq_psum, 1)
                    if runs(edge, u, 1):
                        q, v = n - 1, (u - 1) % QU
                        if u == 0 and edge is None:
                            pe.wait_ge(z_ready, (h + 1) * C)
                        if u == 1 and edge == "first":
                            pe.wait_ge(z_ready, C)
                        pe.wait_ge(xqt_ready, q + 1)
                        since(pe, gate_ready, q)
                        for t in range(QT):
                            last = PE.matmul(psum[:, 2, t * CZ:(t + 1) * CZ], xT2[:, v % 2, t * P:(t + 1) * P],
                                             w_gate[:, :], start=True, stop=True)
                        last.then_inc(g_psum, 1)
                    if runs(edge, u, 2):
                        q, v = n - 2, (u - 2) % QU
                        if u == 2:
                            pe.wait_ge(znt_ready, r + 1)
                        since(pe, gated, q - 1)
                        PE.matmul(psum[:, 4 + v % 2, :], znT[:, v // 2],
                                  w_z[:, (v % 2) * QT:(v % 2 + 1) * QT, :].rearrange("p t c -> p (t c)"),
                                  start=True, stop=True).then_inc(h_psum, 1)
                    if u == 1 and edge != "last":
                        pe.wait_ge(zn_ready, r + 1)
                        if edge is None:
                            pe.wait_ge(yt_ready, n - 5)
                        for g in range(RT // GT):
                            last = PE.transpose(psum[:, 1, g * P:(g + 1) * P],
                                                zn[:, g * GT:(g + 1) * GT, :].rearrange("p s c -> p (s c)"), ident[:, :])
                        last.then_inc(znt_psum, 1)
                    if runs(edge, u, 6):
                        q, v = n - 6, (u - 6) % QU
                        pe.wait_ge(yt_ready, q + 1)
                        if v % 2 == 0:
                            since(pe, logit_ready, (r - 1) * (QU // 2) + u // 2)
                        for t in range(QT):
                            last = PE.matmul(psum[:, 6 - 3 * (v // 2 % 2), (v % 2 * QT + t) * E:(v % 2 * QT + t + 1) * E],
                                             yT[:, t * P:(t + 1) * P], w_exp[:, :], start=True, stop=True)
                        last.then_inc(l_psum, 1)
                    if runs(edge, u, 5):
                        q, v = n - 5, (u - 5) % QU
                        pe.wait_ge(y_ready, q + 1)
                        since(pe, yt_ready, q)
                        if u == 1 and edge != "last":
                            pe.wait_ge(znt_ready, r + 1)
                        for t in range(QT):
                            last = PE.transpose(psum[:, 1, t * P:(t + 1) * P], xq[:, v, t], ident[:, :])
                        last.then_inc(y_psum, 1)

            slabs(pe, fill, body)

            pe.drain()
            pe.sem_inc(ends, 1)
            pe.wait_ge(diag_ready, 1)
            pe.wait_ge(tail_pool, 5)
            for k in range(K // 2):
                last = PE.matmul(psum[:, 0, k * P:(k + 1) * P], ones_m, diag[:, k], start=True, stop=True)
            last.then_inc(tok_row_psum, 1)
            pe.wait_ge(same_ready, 1)
            for t in range(K // 2):
                for s in range(t + 1):
                    last = PE.matmul(psum[:, 5, t:t + 1], same[:, s, t] if s < t else same_before[:, t],
                                     ones_m[:, 0:1], start=(s == 0), stop=(s == t))
            last.then_inc(count_psum, 1)
            pe.wait_ge(rows_ready, 1)
            for k in range(K // 2):
                last = PE.matmul(psum[:, 1, 0:E], rows_n[:, k], pick, start=(k == 0), stop=(k == K // 2 - 1))
            last.then_inc(pooled_psum, 1)
            pe.wait_ge(pooled_ready, 1)
            pe.wait_ge(w1_in, 16 * E)
            for c in range(EC):
                for e in range(c * EG, (c + 1) * EG):
                    j, i = e // 32, e % 32
                    last = PE.matmul(psum[32 * j:32 * (j + 1), 3, :], pooled1[:, j, 32 * i:32 * (i + 1)],
                                     w_sb[:, e], start=(i == 0), stop=(i == 31))
                last.then_inc(h1_done, 1)
            pe.wait_ge(hid_ready, 1)
            for g in range(4):
                last = PE.transpose(psum[:, 2, g * E:(g + 1) * E], hid[0:E, bass.ds(g, P, 4)], ident[0:E, 0:E])
            last.then_inc(ht_psum, 1)
            pe.wait_ge(ht_ready, 1)
            for c in range(EC):
                pe.wait_ge(w2_in[c], 16)
                for e in range(c * EG, (c + 1) * EG):
                    j, i = e // 32, e % 32
                    for g in range(4):
                        last = PE.matmul(psum[32 * j:32 * (j + 1), 4, 0:CZ], hidden4[:, g, j, 32 * i:32 * (i + 1)],
                                         w_sb[:, e, g * CZ:(g + 1) * CZ], start=(i == 0 and g == 0),
                                         stop=(i == 31 and g == 3))
            last.then_inc(o_psum, 1)
            pe.wait_ge(ot_ready, 1)
            PE.matmul(psum[:, 6, 0:CZ], twice[0:E], o_sb[0:E], start=True, stop=True).then_inc(o_psum, 1)
            pe.wait_ge(yadd_ready, 1)
            for t in range(K // 2):
                for s in range(K // 2):
                    last = PE.matmul(psum[:, 7, t * CZ:(t + 1) * CZ], same[:, s, t], y_add[:, s],
                                     start=(s == 0), stop=(s == K // 2 - 1))
            last.then_inc(o_psum, 1)


_INS = ["x", "L0_conv_Wa1", "L0_conv_ba1", "L0_conv_Wa2", "L0_conv_ba2", "L0_conv_Wb1", "L0_conv_bb1",
        "L0_conv_Wb2", "L0_conv_bb2", "L0_conv_ln2_g", "L0_conv_ln2_b", "L0_conv_Wg", "L0_conv_bg",
        "L0_conv_Wz", "L0_conv_bz", "L0_ffn_gate_w", "L0_ffn_gate_b", "L0_ffn_weight1", "L0_ffn_weight2"]


def kernel(**inputs):
    import numpy as _np
    import concourse.bacc as _bacc
    from concourse import mybir as _mybir
    from concourse.bass_utils import run_bass_kernel_spmd as _run

    nc = _bacc.Bacc("TRN2", target_bir_lowering=False, num_devices=1)
    arrays, args = {}, []
    for name in _INS:
        a = _np.ascontiguousarray(inputs[name])
        arrays[f"in_{name}_dram"] = a
        args.append(nc.dram_tensor(f"in_{name}_dram", a.shape, _mybir.dt.from_np(a.dtype), kind="ExternalInput").ap())
    shape = inputs["x"].shape
    args.append(nc.dram_tensor("out_0_dram", shape, _mybir.dt.from_np(_np.dtype("float32")), kind="ExternalOutput").ap())
    build(nc, *args)
    r = _run(nc, [arrays], core_ids=[0])
    return r.results[0]["out_0_dram"]
```
